# Optimizing a Trainium2 kernel written in Bass

```python
import numpy as np
import jax
import jax.numpy as jnp

def _softmax(x, axis=-1):
    return jax.nn.softmax(x, axis=axis)

def _gelu(x):
    return jax.nn.gelu(x, approximate=True)

def _silu(x):
    return jax.nn.silu(x)

def _sigmoid(x):
    return jax.nn.sigmoid(x)

def _layernorm(x, axis=-1, eps=1e-05):
    m = jnp.mean(x, axis=axis, keepdims=True)
    v = jnp.var(x, axis=axis, keepdims=True)
    return (x - m) / jnp.sqrt(v + eps)

def _scatter_add(tgt, idx, src, axis=0):
    return tgt.at[idx].add(src)

def _segment_sum(src, seg, n):
    return jax.ops.segment_sum(src, seg, n)
kernel_name = 'mk_gnn_preln_d4_gnn_r8_a297b7'

def setup_inputs(seed: int=0):
    np.random.seed(seed)
    _w = jnp.asarray

    def _rec_inputs():
        import jax
        import jax.numpy as jnp
        _gk = jax.random.key(seed)
        x = -0.000202 + 1 * jax.random.normal(jax.random.fold_in(_gk, 1), (6250, 128), jnp.float32)
        _s = jax.random.randint(jax.random.fold_in(_gk, 2), (50000,), 0, 6250, jnp.int32)
        _d = jax.random.randint(jax.random.fold_in(_gk, 3), (50000,), 0, 6250, jnp.int32)
        _loop = jnp.arange(6250, dtype=jnp.int32)
        src = jnp.concatenate([_s, _d, _loop])
        dst = jnp.concatenate([_d, _s, _loop])
        _o = jnp.argsort(dst, stable=True)
        src = src[_o]
        dst = dst[_o]
        edge_attr_128 = -5.16925e-05 + 1.00005 * jax.random.normal(jax.random.fold_in(_gk, 13), (106250, 128), jnp.float32)
        edge_attr_64 = -7.08334e-05 + 0.999895 * jax.random.normal(jax.random.fold_in(_gk, 14), (106250, 64), jnp.float32)
        return (x, src, dst, edge_attr_128, edge_attr_64)
    x, src, dst, edge_attr_128, edge_attr_64 = _rec_inputs()

    def _L0_gnn_setup():
        import jax, jax.numpy as jnp
        import numpy as np
        N = 6250
        E = 75000
        HID = 128
        EDIM = 64
        BN_EPS = 1e-05
        key = jax.random.key(seed)
        ks = jax.random.split(key, 10)
        s = 1.0 / np.sqrt(HID)
        se = 1.0 / np.sqrt(EDIM)
        return {'x': jax.random.normal(ks[0], (N, HID), jnp.float32), 'edge_attr': jax.random.normal(ks[1], (E, EDIM), jnp.float32), 'We': jax.random.uniform(ks[2], (EDIM, HID), jnp.float32, -se, se), 'be': jnp.zeros((HID,), jnp.float32), 'W1': jax.random.uniform(ks[3], (HID, HID), jnp.float32, -s, s), 'b1': jnp.zeros((HID,), jnp.float32), 'W2': jax.random.uniform(ks[4], (HID, HID), jnp.float32, -s, s), 'b2': jnp.zeros((HID,), jnp.float32), 'gamma': jnp.ones((HID,), jnp.float32), 'beta': jnp.zeros((HID,), jnp.float32), 'eps': jnp.zeros((), jnp.float32), 'edge_index': jax.random.randint(ks[5], (2, E), 0, N, jnp.int32)}
    _L0_gnn_all = _L0_gnn_setup()
    _L0_gnn_in = {k: v for k, v in _L0_gnn_all.items() if k in ('We', 'be', 'W1', 'b1', 'W2', 'b2', 'gamma', 'beta', 'eps')}
    del _L0_gnn_all

    def _L1_gnn_setup():
        import jax, jax.numpy as jnp
        import numpy as np
        N_NODES = 6250
        N_EDGES = 75000
        D = 128
        key = jax.random.key(seed)
        k1, k2, k3, k4, k5 = jax.random.split(key, 5)
        x = jax.random.normal(k1, (N_NODES, D), dtype=jnp.float32)
        W = jax.random.normal(k2, (D, 2 * D), dtype=jnp.float32) * (1.0 / np.sqrt(2 * D))
        b = jax.random.normal(k3, (D,), dtype=jnp.float32) * 0.01
        src = jax.random.randint(k4, (N_EDGES,), 0, N_NODES, dtype=jnp.int32)
        dst = jax.random.randint(k5, (N_EDGES,), 0, N_NODES, dtype=jnp.int32)
        return {'x': x, 'W': W, 'b': b, 'src': src, 'dst': dst}
    _L1_gnn_all = _L1_gnn_setup()
    _L1_gnn_in = {k: v for k, v in _L1_gnn_all.items() if k in ('W', 'b')}
    del _L1_gnn_all

    def _L2_gnn_setup():
        import jax, jax.numpy as jnp
        import numpy as np
        N, E, D, H = (6250, 100000, 128, 8)
        O = D // H
        NEG_SLOPE = 0.2
        LN_EPS = 1e-05

        def layer_norm(x, g, b):
            mu = jnp.mean(x, axis=-1, keepdims=True)
            var = jnp.mean((x - mu) ** 2, axis=-1, keepdims=True)
            return (x - mu) * jax.lax.rsqrt(var + LN_EPS) * g + b

        def gatv2(x, edge_index, edge_attr, W_l, b_l, W_r, b_r, W_e, att, b_att):
            src, dst = (edge_index[0], edge_index[1])
            xl = (x @ W_l + b_l).reshape(-1, H, O)
            xr = (x @ W_r + b_r).reshape(-1, H, O)
            ee = (edge_attr @ W_e).reshape(-1, H, O)
            m = jax.nn.leaky_relu(xl[src] + xr[dst] + ee, NEG_SLOPE)
            logits = jnp.einsum('eho,ho->eh', m, att)
            lmax = jax.ops.segment_max(logits, dst, num_segments=N)
            exl = jnp.exp(logits - lmax[dst])
            denom = jax.ops.segment_sum(exl, dst, num_segments=N)
            alpha = exl / (denom[dst] + 1e-16)
            msg = xl[src] * alpha[:, :, None]
            out = jax.ops.segment_sum(msg, dst, num_segments=N)
            return out.reshape(-1, H * O) + b_att
        key = jax.random.key(seed)
        ks = jax.random.split(key, 20)
        s = 1.0 / np.sqrt(D)
        sf = 1.0 / np.sqrt(4 * D)
        return {'x': jax.random.normal(ks[0], (N, D), jnp.float32), 'edge_index': jax.random.randint(ks[1], (2, E), 0, N, jnp.int32), 'edge_attr': jax.random.normal(ks[2], (E, D), jnp.float32), 'batch': jnp.zeros((N,), jnp.int32), 'W_l': jax.random.normal(ks[3], (D, H * O), jnp.float32) * s, 'b_l': jnp.zeros((H * O,), jnp.float32), 'W_r': jax.random.normal(ks[4], (D, H * O), jnp.float32) * s, 'b_r': jnp.zeros((H * O,), jnp.float32), 'W_e': jax.random.normal(ks[5], (D, H * O), jnp.float32) * s, 'att': jax.random.normal(ks[6], (H, O), jnp.float32) * (1.0 / np.sqrt(O)), 'b_att': jnp.zeros((H * O,), jnp.float32), 'W1': jax.random.normal(ks[7], (D, 4 * D), jnp.float32) * s, 'b1': jnp.zeros((4 * D,), jnp.float32), 'W2': jax.random.normal(ks[8], (4 * D, D), jnp.float32) * sf, 'b2': jnp.zeros((D,), jnp.float32), 'g1': jnp.ones((D,), jnp.float32), 'be1': jnp.zeros((D,), jnp.float32), 'g2': jnp.ones((D,), jnp.float32), 'be2': jnp.zeros((D,), jnp.float32)}
    _L2_gnn_all = _L2_gnn_setup()
    _L2_gnn_in = {k: v for k, v in _L2_gnn_all.items() if k in ('W_l', 'b_l', 'W_r', 'b_r', 'W_e', 'att', 'b_att', 'W1', 'b1', 'W2', 'b2', 'g1', 'be1', 'g2', 'be2')}
    del _L2_gnn_all

    def _L3_gnn_setup():
        import jax, jax.numpy as jnp
        import numpy as np
        NEG_SLOPE = 0.2

        def _gat_conv(x, edge_index, W, att_src, att_dst, bias, heads, out_ch, concat):
            N = x.shape[0]
            src, dst = (edge_index[0], edge_index[1])
            h = (x @ W).reshape(N, heads, out_ch)
            a_src = jnp.einsum('nhc,hc->nh', h, att_src)
            a_dst = jnp.einsum('nhc,hc->nh', h, att_dst)
            e = a_src[src] + a_dst[dst]
            e = jnp.where(e > 0, e, NEG_SLOPE * e)
            m = jax.ops.segment_max(e, dst, num_segments=N)
            e = jnp.exp(e - m[dst])
            s = jax.ops.segment_sum(e, dst, num_segments=N)
            alpha = e / (s[dst] + 1e-16)
            msg = h[src] * alpha[:, :, None]
            out = jax.ops.segment_sum(msg, dst, num_segments=N)
            if concat:
                out = out.reshape(N, heads * out_ch)
            else:
                out = out.mean(axis=1)
            return out + bias
        key = jax.random.key(seed)
        ks = jax.random.split(key, 12)
        N, E = (12500, 200000)
        dinp, dhid, dout, heads = (128, 32, 128, 4)
        x = jax.random.normal(ks[0], (N, dinp), dtype=jnp.float32)
        a = jax.random.randint(ks[1], (2, E), 0, N, dtype=jnp.int64)
        s1 = 1.0 / np.sqrt(dinp)
        s2 = 1.0 / np.sqrt(dhid * heads)
        return {'x': x, 'a': a, 'W1': jax.random.normal(ks[2], (dinp, heads * dhid), dtype=jnp.float32) * s1, 'att_src1': jax.random.normal(ks[3], (heads, dhid), dtype=jnp.float32) * s1, 'att_dst1': jax.random.normal(ks[4], (heads, dhid), dtype=jnp.float32) * s1, 'b1': jnp.zeros((heads * dhid,), dtype=jnp.float32), 'W2': jax.random.normal(ks[5], (heads * dhid, dout), dtype=jnp.float32) * s2, 'att_src2': jax.random.normal(ks[6], (1, dout), dtype=jnp.float32) * s2, 'att_dst2': jax.random.normal(ks[7], (1, dout), dtype=jnp.float32) * s2, 'b2': jnp.zeros((dout,), dtype=jnp.float32)}
    _L3_gnn_all = _L3_gnn_setup()
    _L3_gnn_in = {k: v for k, v in _L3_gnn_all.items() if k in ('W1', 'att_src1', 'att_dst1', 'b1', 'W2', 'att_src2', 'att_dst2', 'b2')}
    del _L3_gnn_all
    return {'x': x, 'src': src, 'dst': dst, 'edge_attr_128': edge_attr_128, 'edge_attr_64': edge_attr_64, 'L0_gnn_We': _L0_gnn_in['We'], 'L0_gnn_be': _L0_gnn_in['be'], 'L0_gnn_W1': _L0_gnn_in['W1'], 'L0_gnn_b1': _L0_gnn_in['b1'], 'L0_gnn_W2': _L0_gnn_in['W2'], 'L0_gnn_b2': _L0_gnn_in['b2'], 'L0_gnn_gamma': _L0_gnn_in['gamma'], 'L0_gnn_beta': _L0_gnn_in['beta'], 'L0_gnn_eps': _L0_gnn_in['eps'], 'L1_gnn_W': _L1_gnn_in['W'], 'L1_gnn_b': _L1_gnn_in['b'], 'L2_gnn_W_l': _L2_gnn_in['W_l'], 'L2_gnn_b_l': _L2_gnn_in['b_l'], 'L2_gnn_W_r': _L2_gnn_in['W_r'], 'L2_gnn_b_r': _L2_gnn_in['b_r'], 'L2_gnn_W_e': _L2_gnn_in['W_e'], 'L2_gnn_att': _L2_gnn_in['att'], 'L2_gnn_b_att': _L2_gnn_in['b_att'], 'L2_gnn_W1': _L2_gnn_in['W1'], 'L2_gnn_b1': _L2_gnn_in['b1'], 'L2_gnn_W2': _L2_gnn_in['W2'], 'L2_gnn_b2': _L2_gnn_in['b2'], 'L2_gnn_g1': _L2_gnn_in['g1'], 'L2_gnn_be1': _L2_gnn_in['be1'], 'L2_gnn_g2': _L2_gnn_in['g2'], 'L2_gnn_be2': _L2_gnn_in['be2'], 'L3_gnn_W1': _L3_gnn_in['W1'], 'L3_gnn_att_src1': _L3_gnn_in['att_src1'], 'L3_gnn_att_dst1': _L3_gnn_in['att_dst1'], 'L3_gnn_b1': _L3_gnn_in['b1'], 'L3_gnn_W2': _L3_gnn_in['W2'], 'L3_gnn_att_src2': _L3_gnn_in['att_src2'], 'L3_gnn_att_dst2': _L3_gnn_in['att_dst2'], 'L3_gnn_b2': _L3_gnn_in['b2']}

def reference(x, src, dst, edge_attr_128, edge_attr_64, L0_gnn_We, L0_gnn_be, L0_gnn_W1, L0_gnn_b1, L0_gnn_W2, L0_gnn_b2, L0_gnn_gamma, L0_gnn_beta, L0_gnn_eps, L1_gnn_W, L1_gnn_b, L2_gnn_W_l, L2_gnn_b_l, L2_gnn_W_r, L2_gnn_b_r, L2_gnn_W_e, L2_gnn_att, L2_gnn_b_att, L2_gnn_W1, L2_gnn_b1, L2_gnn_W2, L2_gnn_b2, L2_gnn_g1, L2_gnn_be1, L2_gnn_g2, L2_gnn_be2, L3_gnn_W1, L3_gnn_att_src1, L3_gnn_att_dst1, L3_gnn_b1, L3_gnn_W2, L3_gnn_att_src2, L3_gnn_att_dst2, L3_gnn_b2):
    import jax
    import jax.numpy as jnp

    def _L0_gnn_ref(x, edge_attr, We, be, W1, b1, W2, b2, gamma, beta, eps, edge_index):
        import jax, jax.numpy as jnp
        import numpy as np
        N = 6250
        E = 75000
        HID = 128
        EDIM = 64
        BN_EPS = 1e-05
        src, dst = (edge_index[0], edge_index[1])
        msg = jax.nn.relu(x[src] + edge_attr @ We + be)
        aggr = jax.ops.segment_sum(msg, dst, num_segments=N)
        h = (1.0 + eps) * x + aggr
        h = jax.nn.relu(h @ W1 + b1) @ W2 + b2
        mu = jnp.mean(h, axis=0)
        var = jnp.var(h, axis=0)
        h = (h - mu) * jax.lax.rsqrt(var + BN_EPS) * gamma + beta
        return jax.nn.relu(h) + x

    def _L1_gnn_ref(x, W, b, src, dst):
        import jax, jax.numpy as jnp
        import numpy as np
        N_NODES = 6250
        N_EDGES = 75000
        D = 128
        N = x.shape[0]
        neigh_sum = jax.ops.segment_sum(x[src], dst, num_segments=N)
        deg = jax.ops.segment_sum(jnp.ones_like(src, dtype=x.dtype), dst, num_segments=N)
        mean = neigh_sum / jnp.maximum(deg, 1.0)[:, None]
        neigh_agg = jnp.where(deg[:, None] > 0, mean, x)
        h = jnp.concatenate([x, neigh_agg], axis=-1)
        return jax.nn.relu(h @ W.T + b)

    def _L2_gnn_ref(x, edge_index, edge_attr, batch, W_l, b_l, W_r, b_r, W_e, att, b_att, W1, b1, W2, b2, g1, be1, g2, be2):
        import jax, jax.numpy as jnp
        import numpy as np
        N, E, D, H = (6250, 100000, 128, 8)
        O = D // H
        NEG_SLOPE = 0.2
        LN_EPS = 1e-05

        def layer_norm(x, g, b):
            mu = jnp.mean(x, axis=-1, keepdims=True)
            var = jnp.mean((x - mu) ** 2, axis=-1, keepdims=True)
            return (x - mu) * jax.lax.rsqrt(var + LN_EPS) * g + b

        def gatv2(x, edge_index, edge_attr, W_l, b_l, W_r, b_r, W_e, att, b_att):
            src, dst = (edge_index[0], edge_index[1])
            xl = (x @ W_l + b_l).reshape(-1, H, O)
            xr = (x @ W_r + b_r).reshape(-1, H, O)
            ee = (edge_attr @ W_e).reshape(-1, H, O)
            m = jax.nn.leaky_relu(xl[src] + xr[dst] + ee, NEG_SLOPE)
            logits = jnp.einsum('eho,ho->eh', m, att)
            lmax = jax.ops.segment_max(logits, dst, num_segments=N)
            exl = jnp.exp(logits - lmax[dst])
            denom = jax.ops.segment_sum(exl, dst, num_segments=N)
            alpha = exl / (denom[dst] + 1e-16)
            msg = xl[src] * alpha[:, :, None]
            out = jax.ops.segment_sum(msg, dst, num_segments=N)
            return out.reshape(-1, H * O) + b_att
        attn_out = gatv2(x, edge_index, edge_attr, W_l, b_l, W_r, b_r, W_e, att, b_att)
        h = layer_norm(x + attn_out, g1, be1)
        ffn = jax.nn.gelu(h @ W1 + b1, approximate=False) @ W2 + b2
        return layer_norm(h + ffn, g2, be2)

    def _L3_gnn_ref(x, a, W1, att_src1, att_dst1, b1, W2, att_src2, att_dst2, b2):
        import jax, jax.numpy as jnp
        import numpy as np
        NEG_SLOPE = 0.2

        def _gat_conv(x, edge_index, W, att_src, att_dst, bias, heads, out_ch, concat):
            N = x.shape[0]
            src, dst = (edge_index[0], edge_index[1])
            h = (x @ W).reshape(N, heads, out_ch)
            a_src = jnp.einsum('nhc,hc->nh', h, att_src)
            a_dst = jnp.einsum('nhc,hc->nh', h, att_dst)
            e = a_src[src] + a_dst[dst]
            e = jnp.where(e > 0, e, NEG_SLOPE * e)
            m = jax.ops.segment_max(e, dst, num_segments=N)
            e = jnp.exp(e - m[dst])
            s = jax.ops.segment_sum(e, dst, num_segments=N)
            alpha = e / (s[dst] + 1e-16)
            msg = h[src] * alpha[:, :, None]
            out = jax.ops.segment_sum(msg, dst, num_segments=N)
            if concat:
                out = out.reshape(N, heads * out_ch)
            else:
                out = out.mean(axis=1)
            return out + bias
        heads, dhid, dout = (4, 32, 128)
        h = _gat_conv(x, a, W1, att_src1, att_dst1, b1, heads, dhid, concat=True)
        h = jax.nn.elu(h)
        out = _gat_conv(h, a, W2, att_src2, att_dst2, b2, 1, dout, concat=False)
        return jax.nn.elu(out)
    edge_index = jnp.stack([src, dst])
    batch0 = jnp.zeros((6250,), jnp.int32)
    h = jnp.maximum(_layernorm(x, axis=-1), 0.0)
    x = x + _L0_gnn_ref(h, edge_attr_64, L0_gnn_We, L0_gnn_be, L0_gnn_W1, L0_gnn_b1, L0_gnn_W2, L0_gnn_b2, L0_gnn_gamma, L0_gnn_beta, L0_gnn_eps, edge_index)
    h = jnp.maximum(_layernorm(x, axis=-1), 0.0)
    x = x + _L1_gnn_ref(h, L1_gnn_W, L1_gnn_b, src, dst)
    h = jnp.maximum(_layernorm(x, axis=-1), 0.0)
    x = x + _L2_gnn_ref(h, edge_index, edge_attr_128, batch0, L2_gnn_W_l, L2_gnn_b_l, L2_gnn_W_r, L2_gnn_b_r, L2_gnn_W_e, L2_gnn_att, L2_gnn_b_att, L2_gnn_W1, L2_gnn_b1, L2_gnn_W2, L2_gnn_b2, L2_gnn_g1, L2_gnn_be1, L2_gnn_g2, L2_gnn_be2)
    h = jnp.maximum(_layernorm(x, axis=-1), 0.0)
    x = x + _L3_gnn_ref(h, edge_index, L3_gnn_W1, L3_gnn_att_src1, L3_gnn_att_dst1, L3_gnn_b1, L3_gnn_W2, L3_gnn_att_src2, L3_gnn_att_dst2, L3_gnn_b2)
    return x

_drawn_inputs = setup_inputs


def setup_inputs(seed=0):
    import zlib

    import numpy as np

    out = dict(_drawn_inputs(seed))
    spreads = {'L0_gnn_be': (0.0, 0.1),
     'L0_gnn_b1': (0.0, 0.8),
     'L0_gnn_b2': (0.0, 2.0),
     'L0_gnn_gamma': (1.0, 0.2),
     'L0_gnn_beta': (0.0, 0.1),
     'L2_gnn_b_l': (0.0, 0.1),
     'L2_gnn_b_r': (0.0, 2.0),
     'L2_gnn_b_att': (0.0, 0.1),
     'L2_gnn_b1': (0.0, 0.413),
     'L2_gnn_b2': (0.0, 0.268),
     'L2_gnn_g1': (1.0, 0.2),
     'L2_gnn_be1': (0.0, 0.1),
     'L2_gnn_g2': (1.0, 0.2),
     'L2_gnn_be2': (0.0, 0.1),
     'L3_gnn_b1': (0.0, 0.1),
     'L3_gnn_b2': (0.0, 0.1)}
    factors = {'L1_gnn_b': 8.0,
     'L3_gnn_att_src1': 5.048,
     'L3_gnn_att_dst1': 26.94,
     'L3_gnn_att_src2': 8.0,
     'L3_gnn_att_dst2': 134.277,
     'L2_gnn_W_r': 3.265}
    for name, (base, spread) in spreads.items():
        noise = np.random.default_rng([zlib.crc32(name.encode()), seed]).standard_normal(out[name].shape)
        drawn = base * np.exp(spread * noise) if base else spread * noise
        out[name] = jnp.asarray(drawn.astype(out[name].dtype))
    for name, factor in factors.items():
        out[name] = (out[name] * factor).astype(out[name].dtype)
    return out
```

```python
from collections import namedtuple
from contextlib import ExitStack

import concourse.bass as bass
import concourse.mybir as mybir
import numpy as np

F32 = mybir.dt.float32
I32 = mybir.dt.int32
ALU = mybir.AluOpType
ACT = mybir.ActivationFunctionType
AX = mybir.AxisListType.X
DVE = mybir.EngineType.DVE
SP = mybir.EngineType.SP

P = 128
D = 128
N = 6250
E = 106250
TPG = 4
GE = TPG * P
UNROLL = 4
G = -(-E // (GE * UNROLL)) * UNROLL
T = G * TPG
EP = G * GE
CH = -(-(N + P) // GE)
NP = CH * GE
NEG = -3.0e38
LN_EPS = 1e-5
EDGE_STEPS = 4
BOUND = "destinations are node numbers, so a window starts at a column of the aggregate"


def named(**things):
    return namedtuple("Named", things)(**things)


def sems(nc, phase, *names, **slots):
    lists = {n: [nc.alloc_semaphore(f"{phase}_{n}{k}") for k in range(count)] for n, count in slots.items()}
    return named(**{n: nc.alloc_semaphore(f"{phase}_{n}") for n in names}, **lists)


def phase_end(nc, s):
    nc.clear_and_free_semaphores([h for v in s for h in (v if isinstance(v, list) else [v])])
    nc.all_engine_barrier()


def settle(eng):
    eng.nop(nofuse=True)


class At:

    def __init__(self, i, base):
        self.i, self.base = i, base

    def back(self, k):
        return At(self.i, self.base - k)

    def times(self, n, add=0):
        c = n * self.base + add
        return c if self.i is None else self.i * (n * UNROLL) + c

    def uses(self, slots, n=1):
        c = n * (self.base // slots + 1)
        return c if self.i is None else self.i * (n * (UNROLL // slots)) + c

    def slot(self, slots):
        return self.base % slots

    def exists(self):
        return self.i is not None or 0 <= self.base < G


def within(nc, i, low, high):
    return nc.s_assert_within(i, low, high, skip_runtime_bounds_check_because="the loop's own bounds")


def chunks(nc, eng, emit):
    emit(0)
    with eng.Fori(1, CH) as i:
        emit(within(nc, i, 1, CH - 1))


def freed(eng, sem, count):
    if not isinstance(count, int):
        eng.wait_ge(sem, count)


def sweep(nc, eng, first, steady, steady_end, last, emit):
    rounds = (steady_end + 1 - steady) // UNROLL
    for s in range(first, steady):
        emit(At(None, s))
    with eng.Fori(0, rounds) as i:
        i = within(nc, i, 0, rounds - 1)
        for j in range(UNROLL):
            emit(At(i, steady + j))
    for s in range(steady + rounds * UNROLL, last + 1):
        emit(At(None, s))


def wait_past(eng, sem, at, n, add):
    v = at.times(n, add)
    if at.i is not None or v > 0:
        eng.wait_ge(sem, v)


def setup_phase(nc, io, sb):
    s = sems(nc, "setup", "loaded", "prep_loaded", "relative", "starts", "starts_stored", "masked", "folded", "fold_copied",
             "zeroed")
    loads = [
        (sb.x, io.x.rearrange("(b p) f -> p b f", p=P)),
        (sb.ident, io.ident), (sb.iota, io.iota), (sb.mask8, io.mask8), (sb.mask4, io.mask4),
        (sb.expand8, io.expand8), (sb.expand4, io.expand4), (sb.ones_row, io.ones_row),
        (sb.window_row, io.window),
        (sb.L0_We, io.L0_We), (sb.L0_W1, io.L0_W1), (sb.L0_W2, io.L0_W2),
        (sb.L0_b1, io.L0_b1), (sb.L0_b2, io.L0_b2), (sb.L0_gamma, io.L0_gamma), (sb.L0_beta, io.L0_beta),
        (sb.L0_be, io.L0_be.partition_broadcast(P)),
        (sb.L0_eps, io.L0_eps.partition_broadcast(P)),
        (sb.L1_W[:, 0, :], io.L1_WT[0:D]), (sb.L1_W[:, 1, :], io.L1_WT[D:2 * D]),
        (sb.L1_b, io.L1_b.partition_broadcast(P)),
        (sb.L2_Wlr[:, 0:D], io.L2_Wl), (sb.L2_Wlr[:, D:2 * D], io.L2_Wr), (sb.L2_We, io.L2_We),
        (sb.L2_blr[:, 0:D], io.L2_bl.partition_broadcast(P)), (sb.L2_blr[:, D:2 * D], io.L2_br.partition_broadcast(P)),
        (sb.L2_att, io.L2_att.partition_broadcast(P)), (sb.L2_batt, io.L2_batt),
        (sb.L2_W1, io.L2_W1), (sb.L2_b1, io.L2_b1),
        (sb.L2_W2, io.L2_W2.rearrange("(q p) f -> p q f", p=P)),
        (sb.L2_b2, io.L2_b2.partition_broadcast(P)),
        (sb.L2_g1, io.L2_g1.partition_broadcast(P)), (sb.L2_be1, io.L2_be1.partition_broadcast(P)),
        (sb.L2_g2, io.L2_g2.partition_broadcast(P)), (sb.L2_be2, io.L2_be2.partition_broadcast(P)),
        (sb.L3_W1x[:, 0:D], io.L3_W1), (sb.L3_W2x[:, 0:D], io.L3_W2),
        (sb.L3_b1, io.L3_b1), (sb.L3_b2, io.L3_b2),
    ]
    with ExitStack() as ctx:
        def tile(name, shape, dt=F32):
            return ctx.enter_context(nc.sbuf_tensor(f"setup_{name}", shape, dt))[:]

        dst_of = tile("dst_of", [P, T], I32)
        window_all = tile("window_all", [P, T], I32)
        here = tile("here", [P, T], I32)
        before = tile("before", [P, T], I32)
        starts = tile("starts", [P, T])
        tail = tile("tail", [1, 1])
        w1t = tile("w1t", [P, D])
        w2t = tile("w2t", [P, D])
        att1 = tile("att1", [P, 2])
        att2 = tile("att2", [P, 2])
        fold1 = tile("fold1", [P, 8])
        psum = sb.psum
        with nc.Block() as block:
            @block.sync
            def _(sp):
                sp.dma_start(dst_of, io.dst_t).then_inc(s.prep_loaded, 16)
                sp.dma_start(window_all, io.window.partition_broadcast(P)).then_inc(s.prep_loaded, 16)
                sp.dma_start(here, io.dst_row[0:1, 1:EP + 1].rearrange("a (p t) -> (a p) t", p=P)).then_inc(s.prep_loaded, 16)
                sp.dma_start(before, io.dst_row[0:1, 0:EP].rearrange("a (p t) -> (a p) t", p=P)).then_inc(s.prep_loaded, 16)
                sp.dma_start(w1t, io.L3_W1T).then_inc(s.prep_loaded, 16)
                sp.dma_start(w2t, io.L3_W2T).then_inc(s.prep_loaded, 16)
                sp.dma_start(att1, io.L3_att1).then_inc(s.prep_loaded, 16)
                sp.dma_start(att2, io.L3_att2).then_inc(s.prep_loaded, 16)
                for to, of in loads:
                    sp.dma_start(to, of).then_inc(s.loaded, 16)
                sp.wait_ge(s.starts, 2)
                sp.dma_start(io.starts[0:1, 0:EP].rearrange("a (p t) -> (a p) t", p=P), starts).then_inc(s.starts_stored, 16)
                sp.dma_start(io.starts[0:1, EP:EP + 1], tail).then_inc(s.starts_stored, 16)
                sp.wait_ge(s.starts_stored, 32)
                sp.wait_ge(s.loaded, 16 * len(loads))

            @block.vector
            def _(v):
                v.memset(tail, NEG).then_inc(s.starts, 1)
                v.wait_ge(s.prep_loaded, 16 * 8)
                v.tensor_tensor(sb.rel, dst_of, window_all, ALU.subtract).then_inc(s.relative, 1)
                v.tensor_tensor(starts, here, before, ALU.not_equal).then_inc(s.relative, 1)
                v.wait_ge(s.relative, 2)
                v.tensor_scalar(starts, starts, NEG, None, ALU.mult).then_inc(s.starts, 1)
                v.wait_ge(s.loaded, 16 * len(loads))
                v.tensor_scalar(fold1[:, 0:4], sb.mask4, att1[:, 0:1], None, ALU.mult).then_inc(s.masked, 1)
                v.tensor_scalar(fold1[:, 4:8], sb.mask4, att1[:, 1:2], None, ALU.mult).then_inc(s.masked, 1)
                v.wait_ge(s.folded, 1)
                v.tensor_copy(sb.L3_W1x[:, D:D + 8], psum[:, 0, 0:8]).then_inc(s.fold_copied, 1)
                v.tensor_copy(sb.L3_W2x[:, D:D + 2], psum[:, 1, 0:2]).then_inc(s.fold_copied, 1)

            @block.tensor
            def _(pe):
                pe.wait_ge(s.prep_loaded, 16 * 8)
                pe.wait_ge(s.masked, 2)
                pe.matmul(psum[:, 0, 0:8], w1t, fold1, start=True, stop=True)
                pe.matmul(psum[:, 1, 0:2], w2t, att2, start=True, stop=True).then_inc(s.folded, 1)
    phase_end(nc, s)


LN_STEPS = 8


def ln_vector(v, i, steps, std_done, x, w, out, relu, gain=None, shift=None):
    n = LN_STEPS + (0 if relu else 2)
    v.tensor_reduce(w.mean, x, AX, ALU.add).then_inc(steps, 1)
    v.wait_ge(steps, i * n + 1)
    v.tensor_scalar(w.mean, w.mean, 1.0 / D, None, ALU.mult).then_inc(steps, 1)
    v.wait_ge(steps, i * n + 2)
    v.tensor_tensor(w.centred, x, w.mean.unsqueeze(2).broadcast_to([P, TPG, D]), ALU.subtract).then_inc(steps, 1)
    v.wait_ge(steps, i * n + 3)
    v.tensor_tensor(w.square, w.centred, w.centred, ALU.mult).then_inc(steps, 1)
    v.wait_ge(steps, i * n + 4)
    v.tensor_reduce(w.var, w.square, AX, ALU.add).then_inc(steps, 1)
    v.wait_ge(steps, i * n + 5)
    v.tensor_scalar(w.var, w.var, 1.0 / D, LN_EPS, ALU.mult, ALU.add).then_inc(steps, 1)
    v.wait_ge(std_done, i + 1)
    v.reciprocal(w.rstd, w.std).then_inc(steps, 1)
    v.wait_ge(steps, i * n + 7)
    scale = w.rstd.unsqueeze(2).broadcast_to([P, TPG, D])
    if relu:
        v.scalar_tensor_tensor(out, w.centred, 0.0, scale, ALU.max, ALU.mult).then_inc(steps, 1)
        return
    v.tensor_tensor(w.square, w.centred, scale, ALU.mult).then_inc(steps, 1)
    v.wait_ge(steps, i * n + 8)
    v.tensor_tensor(w.square, w.square, gain.unsqueeze(1).broadcast_to([P, TPG, D]), ALU.mult).then_inc(steps, 1)
    v.wait_ge(steps, i * n + 9)
    v.tensor_tensor(out, w.square, shift.unsqueeze(1).broadcast_to([P, TPG, D]), ALU.add).then_inc(steps, 1)


def ln_scalar(act, i, steps, std_done, w, relu):
    act.wait_ge(steps, i * (LN_STEPS + (0 if relu else 2)) + 6)
    act.activation(w.std, w.var, ACT.Sqrt).then_inc(std_done, 1)


def ln_work(tile, name):
    return named(mean=tile(name + "_mean", [P, TPG]), var=tile(name + "_var", [P, TPG]),
                           std=tile(name + "_std", [P, TPG]), rstd=tile(name + "_rstd", [P, TPG]),
                           centred=tile(name + "_centred", [P, TPG, D]), square=tile(name + "_square", [P, TPG, D]))


def blocks_to_features(pe, out, blocks, ident):
    for b in range(TPG):
        last = pe.transpose(out[:, b * P:(b + 1) * P], blocks[:, b, :], ident)
    return last


def nodes_of(i):
    return bass.ds(i * GE, GE)


def table_rows(table, i):
    return table[nodes_of(i), :].rearrange("(b p) f -> p b f", p=P)


def norm0_phase(nc, io, sb):
    s = sems(nc, "norm0", "ln_steps", "ln_std", "transposed", "kept", "rows", "stored")
    with ExitStack() as ctx:
        def tile(name, shape, dt=F32):
            return ctx.enter_context(nc.sbuf_tensor(f"norm0_{name}", shape, dt))[:]

        w = ln_work(tile, "ln")
        h = tile("h", [P, TPG, D])
        rows = tile("rows", [P, TPG, D])
        with nc.Block() as block:
            @block.vector
            def _(v):
                def chunk(i):
                    freed(v, s.transposed, i)
                    settle(v)
                    ln_vector(v, i, s.ln_steps, s.ln_std, sb.x[:, bass.ds(i * TPG, TPG), :], w, h, True)
                    v.wait_ge(s.ln_steps, i * LN_STEPS + 8)
                    freed(v, s.stored, i * 16)
                    v.tensor_tensor(rows, h, sb.L0_be.unsqueeze(1).broadcast_to([P, TPG, D]), ALU.add).then_inc(s.rows, 1)

                chunks(nc, v, chunk)

            @block.scalar
            def _(act):
                def chunk(i):
                    ln_scalar(act, i, s.ln_steps, s.ln_std, w, True)
                    act.wait_ge(s.transposed, i + 1)
                    act.activation(sb.hT[:, nodes_of(i)], sb.psum[:, 0, :], ACT.Copy).then_inc(s.kept, 1)

                chunks(nc, act, chunk)

            @block.tensor
            def _(pe):
                def chunk(i):
                    pe.wait_ge(s.ln_steps, i * LN_STEPS + 8)
                    freed(pe, s.kept, i)
                    blocks_to_features(pe, sb.psum[:, 0, :], h, sb.ident).then_inc(s.transposed, 1)

                chunks(nc, pe, chunk)

            @block.sync
            def _(sp):
                def chunk(i):
                    sp.wait_ge(s.rows, i + 1)
                    sp.dma_start(table_rows(io.table0, i), rows).then_inc(s.stored, 16)

                chunks(nc, sp, chunk)
                sp.wait_ge(s.stored, 16 * CH)
    phase_end(nc, s)


def edge_phase(nc, io, sb, layer):
    H = {0: 0, 1: 0, 2: 8, 3: 4, 4: 1}[layer]
    soft = H > 0
    weights = layer > 0
    attr = {0: io.ea64T, 2: io.ea128T}.get(layer)
    table, width = {0: (io.table0, D), 1: (io.table1, D), 2: (io.table2, D),
                    3: (io.table3, D + 4), 4: (io.table4, D + 1)}[layer]
    dst_table, dst_width = {2: (io.xr_table, D), 3: (io.adst3, 4), 4: (io.adst4, 2)}.get(layer, (None, 0))
    expand = {2: sb.expand8, 3: sb.expand4, 4: sb.ones_row}.get(layer)
    names = "zeroed onehot edge_term added relued scattered rescaled order".split()
    if soft:
        names += ("onehotT_psum onehotT linear logits logits_lane running lanes maxima_psum factor_log factor "
                  "factor_copied shifted weights relu message").split()
    s = sems(nc, f"edges{layer}", *names, indices=4, gathered=4, attr=2, dst_rows=2, starts=2)
    rows_read = {0: s.added, 1: s.scattered}.get(layer) if not soft else s.message

    with ExitStack() as ctx:
        def tile(name, shape, dt=F32):
            return ctx.enter_context(nc.sbuf_tensor(f"edges{layer}_{name}", shape, dt))[:]

        idx = tile("idx", [P, 4, TPG], I32)
        rows = tile("rows", [P, 4, TPG, width])
        onehot = tile("onehot", [P, 4, TPG, P])
        message = tile("message", [P, 2, TPG, D])
        if attr is not None:
            attrs = tile("attrs", [attr.shape[0], 2, GE])
        if layer in (0, 2):
            term = tile("term", [P, 2, TPG, D])
        if layer == 2:
            relued = tile("relued", [P, TPG, D])
        if layer == 1:
            ones = tile("ones", [P, D])
        if soft:
            onehotT = tile("onehotT", [P, 2, GE])
            dst_rows = tile("dst_rows", [P, 2, TPG, dst_width])
            starts = tile("seg_starts", [H, 2, GE + 1])
            linear = tile("linear", [P, TPG, H])
            logits = tile("logits", [P, 2, TPG, H])
            running = tile("running", [H, 2, GE])
            maxima = tile("maxima", [H, 2, GE])
            factor_log = tile("factor_log", [H, 2])
            factor = tile("factor", [H, 2])
            factor_of = tile("factor_of", [P, 2])
            shifted = tile("shifted", [P, TPG, H])
            weight = tile("weight", [P, 2, TPG, H])
            weight_of = tile("weight_of", [P, 2, TPG, D])
        term_bank = sb.psum[:, 0, :]
        onehotT_bank = sb.psum[:, 1, :]
        lane_bank = sb.psum[:, 2, :]
        maxima_bank = sb.psum[:, 3, :]
        windows = [sb.psum[:, 4 + 2 * k:6 + 2 * k, :].rearrange("p a (t w n) -> p (a t) w n", t=2, w=2) for k in range(2)]
        ORDER = 4 + soft

        with nc.Block() as block:
            @block.sync
            def _(sp):
                def load(g):
                    sp_idx = g.slot(4)
                    if g.i is not None:
                        sp.wait_ge(s.gathered[sp_idx], g.back(4).uses(4, 16 * TPG))
                    sp.dma_start(idx[:, sp_idx, :], io.src_g[bass.ds(g.times(1), 1)].rearrange("a p t -> (a p) t")).then_inc(s.indices[sp_idx], 16)
                    if attr is not None:
                        wait_past(sp, s.edge_term, g, 1, -1)
                        sp.dma_start(attrs[:, g.slot(2), :], attr[:, bass.ds(g.times(GE), GE)]).then_inc(s.attr[g.slot(2)], 16)
                    if soft:
                        if attr is None:
                            wait_past(sp, s.edge_term, g, 1, -1)
                        _, at = nc.values_load_multi_w_load_instructions(
                            sb.window_row[0:1, bass.ds(g.times(TPG), TPG)], engines=[SP], min_val=0, max_val=N,
                            skip_runtime_bounds_check_because=BOUND)
                        for t in range(TPG):
                            sp.dma_start(dst_rows[:, g.slot(2), t, :], dst_table[bass.ds(at[t], P), :]).then_inc(s.dst_rows[g.slot(2)], 16)
                        wait_past(sp, s.lanes, g, 1, -1)
                        sp.dma_start(starts[:, g.slot(2), :],
                                     io.starts[0:1, bass.ds(g.times(GE), GE + 1)].rearrange("a n -> (a n)").partition_broadcast(H)).then_inc(s.starts[g.slot(2)], 16)

                sweep(nc, sp, 0, 4, G - 1, G - 1, load)

            @block.gpsimd
            def _(pool):
                def gather(g):
                    k = g.slot(4)
                    if g.i is not None:
                        pool.wait_ge(rows_read, g.times(1, -3))
                    pool.wait_ge(s.indices[k], g.uses(4, 16))
                    settle(pool)
                    for t in range(TPG):
                        pool.indirect_dma_start(rows[:, k, t, :], None, table,
                                                bass.IndirectOffsetOnAxis(idx[:, k, t:t + 1], 0)).then_inc(s.gathered[k], 16)

                sweep(nc, pool, 0, 4, G - 1, G - 1, gather)

            @block.scalar
            def _(act):
                def step(t):
                    g = t.back(1)
                    if g.exists() and layer == 0:
                        act.wait_ge(s.added, g.times(1, 1))
                        wait_past(act, s.scattered, g, 1, -1)
                        act.activation(message[:, g.slot(2)], term[:, g.slot(2)], ACT.Relu).then_inc(s.relued, 1)
                    if not soft:
                        return
                    g = t
                    if g.exists():
                        act.wait_ge(s.onehotT_psum, g.times(1, 1))
                        wait_past(act, s.edge_term, g, 1, -1)
                        act.activation(onehotT[:, g.slot(2)], onehotT_bank, ACT.Copy).then_inc(s.onehotT, 1)
                    g = t.back(1)
                    if g.exists() and layer == 2:
                        act.wait_ge(s.added, g.times(1, 1))
                        wait_past(act, s.logits, g, 1, 0)
                        act.activation(relued, term[:, g.slot(2)], ACT.Relu, scale=0.8).then_inc(s.relu, 1)
                    g = t.back(2)
                    if g.exists():
                        act.wait_ge(s.factor_log, g.times(1, 1))
                        wait_past(act, s.maxima_psum, g, 1, -1)
                        act.activation(factor[:, g.slot(2):g.slot(2) + 1], factor_log[:, g.slot(2):g.slot(2) + 1], ACT.Exp).then_inc(s.factor, 1)
                        act.wait_ge(s.shifted, g.times(1, 1))
                        wait_past(act, s.scattered, g, 1, -1)
                        act.activation(weight[:, g.slot(2)], shifted, ACT.Exp).then_inc(s.weights, 1)
                        act.wait_ge(s.weights, g.times(1, 1))
                        act.activation(weight_of[:, g.slot(2)].rearrange("p t (h c) -> p t h c", h=H),
                                       weight[:, g.slot(2)].unsqueeze(3).broadcast_to([P, TPG, H, D // H]), ACT.Copy).then_inc(s.linear, 1)

                sweep(nc, act, -1, 7, G - 2, G + 2, step)

            @block.tensor
            def _(pe):
                def step(t):
                    g = t
                    if g.exists() and soft:
                        pe.wait_ge(s.onehot, g.times(1, 1))
                        wait_past(pe, s.onehotT, g, 1, 0)
                        for k in range(TPG):
                            last = pe.transpose(onehotT_bank[:, k * P:(k + 1) * P], onehot[:, g.slot(4), k], sb.ident)
                        last.then_inc(s.onehotT_psum, 1)
                    g = t.back(2)
                    if g.exists() and soft:
                        pe.wait_ge(s.lanes, g.times(1, 1))
                        wait_past(pe, s.shifted, g, 1, 0)
                        settle(pe)
                        for k in range(TPG):
                            pe.transpose(maxima_bank[:, k * H:(k + 1) * H], maxima[:, g.slot(2), k * P:(k + 1) * P], sb.ident[0:H, 0:H])
                        pe.wait_ge(s.factor, g.times(1, 1))
                        pe.matmul(maxima_bank[:, 64:65], expand, factor[:, g.slot(2):g.slot(2) + 1], start=True, stop=True).then_inc(s.maxima_psum, 1)
                    g = t
                    if g.exists() and layer != 1:
                        wait_past(pe, s.added, g, 1, 0)
                        if attr is not None:
                            pe.wait_ge(s.attr[g.slot(2)], g.uses(2, 16))
                        if soft:
                            pe.wait_ge(s.dst_rows[g.slot(2)], g.uses(2, 16 * TPG))
                            pe.wait_ge(s.onehotT, g.times(1, 1))
                        W = D if layer in (0, 2) else H
                        for k in range(TPG):
                            out = term_bank[:, k * W:(k + 1) * W]
                            if attr is not None:
                                last = pe.matmul(out, attrs[:, g.slot(2), k * P:(k + 1) * P], sb.L0_We if layer == 0 else sb.L2_We,
                                                 start=True, stop=not soft)
                            if soft:
                                last = pe.matmul(out, onehotT[:, g.slot(2), k * P:(k + 1) * P], dst_rows[:, g.slot(2), k, dst_width - W:dst_width],
                                                 start=attr is None, stop=True)
                        last.then_inc(s.edge_term, 1)
                    g = t.back(1)
                    if g.exists() and soft:
                        pe.wait_ge(s.logits, g.times(1, 1))
                        wait_past(pe, s.running, g, 1, 0)
                        for k in range(TPG):
                            last = pe.transpose(lane_bank[0:H, k * P:(k + 1) * P], logits[:, g.slot(2), k, :], sb.ident)
                        last.then_inc(s.logits_lane, 1)
                    g = t.back(2)
                    if g.exists():
                        wait_past(pe, s.order, g, ORDER, 1 + soft - ORDER)
                        pe.wait_ge(s.onehot, g.times(1, 1))
                        if soft:
                            pe.wait_ge(s.message, g.times(1, 1))
                            pe.wait_ge(s.linear, g.times(1, 1))
                        elif layer == 0:
                            pe.wait_ge(s.relued, g.times(1, 1))
                        else:
                            pe.wait_ge(s.zeroed, 1)
                            pe.wait_ge(s.gathered[g.slot(4)], g.uses(4, 16 * TPG))
                        for k in range(TPG):
                            what = rows[:, g.slot(4), k, :] if layer == 1 else message[:, g.slot(2), k, :]
                            last = pe.matmul(windows[g.slot(2)][:, k, 0, :], what, onehot[:, g.slot(4), k], start=True, stop=True)
                            if weights:
                                every = weight_of[:, g.slot(2), k, :] if soft else ones
                                last = pe.matmul(windows[g.slot(2)][:, k, 1, :], every, onehot[:, g.slot(4), k], start=True, stop=True)
                        last.then_inc(s.scattered, 1)

                sweep(nc, pe, -1, 7, G - 2, G + 2, step)

            @block.vector
            def _(v):
                v.memset(sb.sums, 0.0).then_inc(s.order, 1)
                if layer == 1:
                    v.memset(ones, 1.0).then_inc(s.zeroed, 1)
                if soft:
                    v.memset(running[:, 1, :], NEG).then_inc(s.order, 1)
                first = 1 + soft
                v.wait_ge(s.order, first)

                def step(t):
                    g3 = t.back(3)
                    if g3.exists():
                        _, at = nc.values_load_multi_w_load_instructions(
                            sb.window_row[0:1, bass.ds(g3.times(TPG), TPG)], engines=[DVE], min_val=0, max_val=N,
                            skip_runtime_bounds_check_because=BOUND)
                    g = t.back(1)
                    if g.exists() and layer in (0, 2):
                        v.wait_ge(s.edge_term, g.times(1, 1))
                        v.wait_ge(s.gathered[g.slot(4)], g.uses(4, 16 * TPG))
                        if layer == 0:
                            wait_past(v, s.relued, g, 1, -1)
                        else:
                            wait_past(v, s.logits, g, 1, -1)
                        v.tensor_tensor(term[:, g.slot(2)], term_bank.rearrange("p (t n) -> p t n", t=TPG), rows[:, g.slot(4)], ALU.add).then_inc(s.added, 1)
                    g = t.back(2)
                    if g.exists() and soft:
                        v.wait_ge(s.logits_lane, g.times(1, 1))
                        v.wait_ge(s.starts[g.slot(2)], g.uses(2, 16))
                        wait_past(v, s.lanes, g, 1, 0)
                        before = running[:, 1 - g.slot(2), GE - 1:GE]
                        v.tensor_tensor_scan(running[:, g.slot(2)], starts[:, g.slot(2), 0:GE], lane_bank[0:H], before,
                                             ALU.add, ALU.max).then_inc(s.running, 1)
                        v.wait_ge(s.running, g.times(1, 1))
                        wait_past(v, s.maxima_psum, g, 1, -1)
                        v.tensor_tensor_scan(maxima[:, g.slot(2), ::-1], starts[:, g.slot(2), GE:0:-1], running[:, g.slot(2), ::-1],
                                             NEG, ALU.add, ALU.max).then_inc(s.lanes, 1)
                        v.wait_ge(s.lanes, g.times(1, 1))
                        wait_past(v, s.factor, g, 1, -1)
                        v.tensor_scalar(factor_log[:, g.slot(2):g.slot(2) + 1], before, maxima[:, g.slot(2), 0:1], 0.0,
                                        ALU.subtract, ALU.min).then_inc(s.factor_log, 1)
                    g = t.back(1)
                    if g.exists() and soft:
                        wait_past(v, s.shifted, g, 1, -1)
                        lg = logits[:, g.slot(2)]
                        if layer == 2:
                            v.wait_ge(s.relu, g.times(1, 1))
                            v.scalar_tensor_tensor(term[:, g.slot(2)], term[:, g.slot(2)], 0.2, relued, ALU.mult, ALU.add).then_inc(s.rescaled, 1)
                            v.wait_ge(s.rescaled, g.times(2, 1))
                            v.tensor_tensor(term[:, g.slot(2)], term[:, g.slot(2)], sb.L2_att.unsqueeze(1).broadcast_to([P, TPG, D]), ALU.mult).then_inc(s.rescaled, 1)
                            v.wait_ge(s.rescaled, g.times(2, 2))
                            v.tensor_reduce(lg, term[:, g.slot(2)].rearrange("p t (h c) -> p t h c", h=H), AX, ALU.add).then_inc(s.logits, 1)
                        else:
                            v.wait_ge(s.edge_term, g.times(1, 1))
                            v.wait_ge(s.gathered[g.slot(4)], g.uses(4, 16 * TPG))
                            wait_past(v, s.logits, g, 1, 0)
                            v.tensor_tensor(linear, term_bank[:, 0:TPG * H].rearrange("p (t h) -> p t h", t=TPG),
                                            rows[:, g.slot(4), :, D:D + H], ALU.add).then_inc(s.added, 1)
                            v.wait_ge(s.added, g.times(1, 1))
                            v.scalar_tensor_tensor(lg, linear, 0.2, linear, ALU.mult, ALU.max).then_inc(s.logits, 1)
                    g = t.back(2)
                    if g.exists() and soft:
                        v.wait_ge(s.maxima_psum, g.times(1, 1))
                        wait_past(v, s.weights, g, 1, 0)
                        wait_past(v, s.order, g, ORDER, 1 + soft - ORDER)
                        v.tensor_copy(factor_of[:, g.slot(2):g.slot(2) + 1], maxima_bank[:, 64:65]).then_inc(s.factor_copied, 1)
                        v.tensor_tensor(shifted, logits[:, g.slot(2)], maxima_bank[:, 0:TPG * H].rearrange("p (t h) -> p t h", t=TPG),
                                        ALU.subtract).then_inc(s.shifted, 1)
                    g = At(t.i, t.base + 1)
                    if g.exists():
                        wait_past(v, s.scattered, g, 1, -3)
                        v.tensor_tensor(onehot[:, g.slot(4)], sb.iota.unsqueeze(1).broadcast_to([P, TPG, P]),
                                        sb.rel[:, bass.ds(g.times(TPG), TPG)].unsqueeze(2).broadcast_to([P, TPG, P]), ALU.is_equal).then_inc(s.onehot, 1)
                    g = t.back(2)
                    if g.exists() and soft:
                        v.wait_ge(s.weights, g.times(1, 1))
                        wait_past(v, s.scattered, g, 1, -1)
                        v.tensor_tensor(message[:, g.slot(2)].rearrange("p t (h c) -> p t h c", h=H),
                                        rows[:, g.slot(4), :, 0:D].rearrange("p t (h c) -> p t h c", h=H),
                                        weight[:, g.slot(2)].unsqueeze(3).broadcast_to([P, TPG, H, D // H]), ALU.mult).then_inc(s.message, 1)
                    g = g3
                    if g.exists():
                        v.wait_ge(s.scattered, g.times(1, 1))
                        wait_past(v, s.order, g, ORDER, first)
                        k0 = 0
                        if soft:
                            column = sb.sums[:, :, bass.ds(at[0], 1)]
                            v.wait_ge(s.factor_copied, g.times(1, 1))
                            v.tensor_scalar(column, column, factor_of[:, g.slot(2):g.slot(2) + 1], None, ALU.mult).then_inc(s.order, 1)
                            v.wait_ge(s.order, g.times(ORDER, first + 1))
                            k0 = 1
                        for k in range(TPG):
                            W = 2 if weights else 1
                            to = sb.sums[:, 0:W, bass.ds(at[k], P)]
                            v.tensor_tensor(to, to, windows[g.slot(2)][:, k, 0:W, :], ALU.add).then_inc(s.order, 1)
                            if k < TPG - 1:
                                v.wait_ge(s.order, g.times(ORDER, first + k0 + k + 1))

                sweep(nc, v, -1, 7, G - 2, G + 2, step)
    phase_end(nc, s)


def mlp0_phase(nc, io, sb):
    s = sems(nc, "mlp0", "scale", "in_", "up", "up_done", "down", "down_done", "stat", "act_stat")
    with ExitStack() as ctx:
        def tile(name, shape, dt=F32):
            return ctx.enter_context(nc.sbuf_tensor(f"mlp0_{name}", shape, dt))[:]

        one_eps = tile("one_eps", [P, 1])
        hin = tile("hin", [P, 2, GE])
        mid = tile("mid", [P, 2, GE])
        square = tile("square", [P, N])
        st = tile("st", [P, 8])
        y = sb.sums[:, 1, :]
        with nc.Block() as block:
            @block.vector
            def _(v):
                v.tensor_scalar(one_eps, sb.L0_eps, 1.0, None, ALU.add).then_inc(s.scale, 1)
                v.wait_ge(s.scale, 1)
                for c in range(CH):
                    if c >= 2:
                        v.wait_ge(s.up, c - 1)
                    cols = slice(c * GE, (c + 1) * GE)
                    v.scalar_tensor_tensor(hin[:, c % 2], sb.hT[:, cols], one_eps, sb.sums[:, 0, cols], ALU.mult, ALU.add).then_inc(s.in_, 1)
                v.wait_ge(s.down_done, CH)
                k = 0
                v.tensor_reduce(st[:, 0:1], y[:, 0:N], AX, ALU.add).then_inc(s.stat, 1)
                v.wait_ge(s.stat, 1)
                v.tensor_scalar(st[:, 1:2], st[:, 0:1], -1.0 / N, None, ALU.mult).then_inc(s.stat, 1)
                v.wait_ge(s.act_stat, 1)
                v.tensor_scalar(st[:, 3:4], st[:, 2:3], 1.0 / N, LN_EPS, ALU.mult, ALU.add).then_inc(s.stat, 1)
                v.wait_ge(s.act_stat, 2)
                v.reciprocal(st[:, 5:6], st[:, 4:5]).then_inc(s.stat, 1)
                v.wait_ge(s.stat, 4)
                v.tensor_tensor(sb.bn_scale, st[:, 5:6], sb.L0_gamma, ALU.mult).then_inc(s.stat, 1)
                v.wait_ge(s.stat, 5)
                v.scalar_tensor_tensor(sb.bn_shift, sb.bn_scale, st[:, 1:2], sb.L0_beta, ALU.mult, ALU.add).then_inc(s.stat, 1)

            @block.tensor
            def _(pe):
                for c in range(CH):
                    pe.wait_ge(s.in_, c + 1)
                    if c >= 2:
                        pe.wait_ge(s.up_done, c - 1)
                    pe.matmul(sb.psum[:, c % 2, :], sb.L0_W1, hin[:, c % 2], start=True, stop=True).then_inc(s.up, 1)
                    pe.wait_ge(s.up_done, c + 1)
                    if c >= 2:
                        pe.wait_ge(s.down_done, c - 1)
                    pe.matmul(sb.psum[:, 2 + c % 2, :], sb.L0_W2, mid[:, c % 2], start=True, stop=True).then_inc(s.down, 1)

            @block.scalar
            def _(act):
                for c in range(CH):
                    act.wait_ge(s.up, c + 1)
                    if c >= 2:
                        act.wait_ge(s.down, c - 1)
                    act.activation(mid[:, c % 2], sb.psum[:, c % 2, :], ACT.Relu, bias=sb.L0_b1).then_inc(s.up_done, 1)
                    act.wait_ge(s.down, c + 1)
                    act.activation(y[:, c * GE:(c + 1) * GE], sb.psum[:, 2 + c % 2, :], ACT.Identity, bias=sb.L0_b2).then_inc(s.down_done, 1)
                act.wait_ge(s.stat, 2)
                act.wait_ge(s.down_done, CH)
                act.activation(square, y[:, 0:N], ACT.Square, bias=st[:, 1:2], accum_out=st[:, 2:3]).then_inc(s.act_stat, 1)
                act.wait_ge(s.stat, 3)
                act.activation(st[:, 4:5], st[:, 3:4], ACT.Sqrt).then_inc(s.act_stat, 1)
    phase_end(nc, s)


def norm1_phase(nc, io, sb):
    s = sems(nc, "norm1", "bn", "plus_h", "back", "x_new", "ln_steps", "ln_std", "transposed", "kept", "stored")
    with ExitStack() as ctx:
        def tile(name, shape, dt=F32):
            return ctx.enter_context(nc.sbuf_tensor(f"norm1_{name}", shape, dt))[:]

        w = ln_work(tile, "ln")
        h = tile("h", [P, TPG, D])
        z = tile("z", [P, GE])
        zh = tile("zh", [P, GE])
        with nc.Block() as block:
            @block.scalar
            def _(act):
                def chunk(i):
                    freed(act, s.plus_h, i)
                    act.activation(z, sb.sums[:, 1, nodes_of(i)], ACT.Relu, bias=sb.bn_shift, scale=sb.bn_scale).then_inc(s.bn, 1)
                    ln_scalar(act, i, s.ln_steps, s.ln_std, w, True)
                    act.wait_ge(s.transposed, i + 1)
                    act.activation(sb.hT[:, nodes_of(i)], sb.psum[:, 1, :], ACT.Copy).then_inc(s.kept, 1)

                chunks(nc, act, chunk)

            @block.vector
            def _(v):
                def chunk(i):
                    x = sb.x[:, bass.ds(i * TPG, TPG), :]
                    v.wait_ge(s.bn, i + 1)
                    freed(v, s.back, i)
                    v.tensor_tensor(zh, z, sb.hT[:, nodes_of(i)], ALU.add).then_inc(s.plus_h, 1)
                    v.wait_ge(s.back, i + 1)
                    v.tensor_tensor(x, x, sb.psum[:, 0, :].rearrange("p (b f) -> p b f", b=TPG), ALU.add).then_inc(s.x_new, 1)
                    v.wait_ge(s.x_new, i + 1)
                    freed(v, s.transposed, i)
                    freed(v, s.stored, i * 16)
                    settle(v)
                    ln_vector(v, i, s.ln_steps, s.ln_std, x, w, h, True)

                chunks(nc, v, chunk)

            @block.tensor
            def _(pe):
                def chunk(i):
                    pe.wait_ge(s.plus_h, i + 1)
                    freed(pe, s.x_new, i)
                    for b in range(TPG):
                        last = pe.transpose(sb.psum[:, 0, b * P:(b + 1) * P], zh[:, b * P:(b + 1) * P], sb.ident)
                    last.then_inc(s.back, 1)
                    pe.wait_ge(s.ln_steps, i * LN_STEPS + 8)
                    freed(pe, s.kept, i)
                    blocks_to_features(pe, sb.psum[:, 1, :], h, sb.ident).then_inc(s.transposed, 1)

                chunks(nc, pe, chunk)

            @block.sync
            def _(sp):
                def chunk(i):
                    sp.wait_ge(s.ln_steps, i * LN_STEPS + 8)
                    sp.dma_start(table_rows(io.table1, i), h).then_inc(s.stored, 16)

                chunks(nc, sp, chunk)
                sp.wait_ge(s.stored, 16 * CH)
    phase_end(nc, s)


def layer1_phase(nc, io, sb):
    s = sems(nc, "layer1", "deg", "inv", "mean", "lonely", "neigh", "h_copied", "lin", "biased", "x_new", "ln_steps", "ln_std",
             "transposed", "kept", "copied", "proj", "rows", "stored")
    with ExitStack() as ctx:
        def tile(name, shape, dt=F32):
            return ctx.enter_context(nc.sbuf_tensor(f"layer1_{name}", shape, dt))[:]

        w = ln_work(tile, "ln")
        deg = tile("deg", [P, GE])
        inv = tile("inv", [P, GE])
        lonely = tile("lonely", [P, GE])
        neigh = tile("neigh", [P, GE])
        hs = tile("hs", [P, GE])
        lin = tile("lin", [P, TPG, D])
        h = tile("h", [P, TPG, D])
        hs2 = tile("hs2", [P, GE])
        rows = tile("rows", [P, TPG, 2 * D])
        proj = sb.psum[:, 2:4, :].rearrange("p a (b f) -> p (a b) f", b=2)
        with nc.Block() as block:
            @block.vector
            def _(v):
                def chunk(i):
                    x = sb.x[:, bass.ds(i * TPG, TPG), :]
                    freed(v, s.neigh, i)
                    v.tensor_scalar(deg, sb.sums[:, 1, nodes_of(i)], 1.0, None, ALU.max).then_inc(s.deg, 1)
                    v.scalar_tensor_tensor(lonely, sb.sums[:, 1, nodes_of(i)], 0.0, sb.hT[:, nodes_of(i)], ALU.is_equal, ALU.mult).then_inc(s.lonely, 1)
                    v.wait_ge(s.deg, i + 1)
                    v.reciprocal(inv, deg).then_inc(s.inv, 1)
                    freed(v, s.lin, i)
                    v.wait_ge(s.inv, i + 1)
                    v.tensor_tensor(inv, inv, sb.sums[:, 0, nodes_of(i)], ALU.mult).then_inc(s.mean, 1)
                    v.wait_ge(s.mean, i + 1)
                    v.wait_ge(s.lonely, i + 1)
                    v.tensor_tensor(neigh, inv, lonely, ALU.add).then_inc(s.neigh, 1)
                    v.wait_ge(s.lin, i + 1)
                    v.tensor_tensor(lin, sb.psum[:, 0, :].rearrange("p (b f) -> p b f", b=TPG),
                                    sb.L1_b.unsqueeze(1).broadcast_to([P, TPG, D]), ALU.add).then_inc(s.biased, 1)
                    v.wait_ge(s.biased, i + 1)
                    v.scalar_tensor_tensor(x, lin, 0.0, x, ALU.max, ALU.add).then_inc(s.x_new, 1)
                    v.wait_ge(s.x_new, i + 1)
                    freed(v, s.transposed, i)
                    settle(v)
                    ln_vector(v, i, s.ln_steps, s.ln_std, x, w, h, True)
                    v.wait_ge(s.proj, i + 1)
                    freed(v, s.stored, i * 32)
                    v.tensor_tensor(rows, proj, sb.L2_blr.unsqueeze(1).broadcast_to([P, TPG, 2 * D]), ALU.add).then_inc(s.rows, 1)

                chunks(nc, v, chunk)

            @block.scalar
            def _(act):
                def chunk(i):
                    freed(act, s.lin, i)
                    act.activation(hs, sb.hT[:, nodes_of(i)], ACT.Copy).then_inc(s.h_copied, 1)
                    ln_scalar(act, i, s.ln_steps, s.ln_std, w, True)
                    act.wait_ge(s.transposed, i + 1)
                    act.wait_ge(s.lonely, i + 1)
                    act.wait_ge(s.h_copied, i + 1)
                    settle(act)
                    act.activation(sb.hT[:, nodes_of(i)], sb.psum[:, 1, :], ACT.Copy).then_inc(s.kept, 1)
                    freed(act, s.proj, i)
                    act.activation(hs2, sb.psum[:, 1, :], ACT.Copy).then_inc(s.copied, 1)

                chunks(nc, act, chunk)

            @block.tensor
            def _(pe):
                def chunk(i):
                    pe.wait_ge(s.neigh, i + 1)
                    pe.wait_ge(s.h_copied, i + 1)
                    freed(pe, s.biased, i)
                    for b in range(TPG):
                        cols = slice(b * P, (b + 1) * P)
                        pe.matmul(sb.psum[:, 0, cols], hs[:, cols], sb.L1_W[:, 0, :], start=True, stop=False)
                        last = pe.matmul(sb.psum[:, 0, cols], neigh[:, cols], sb.L1_W[:, 1, :], start=False, stop=True)
                    last.then_inc(s.lin, 1)
                    pe.wait_ge(s.ln_steps, i * LN_STEPS + 8)
                    freed(pe, s.copied, i)
                    blocks_to_features(pe, sb.psum[:, 1, :], h, sb.ident).then_inc(s.transposed, 1)
                    pe.wait_ge(s.copied, i + 1)
                    freed(pe, s.rows, i)
                    for b in range(TPG):
                        last = pe.matmul(proj[:, b, :], hs2[:, b * P:(b + 1) * P], sb.L2_Wlr, start=True, stop=True)
                    last.then_inc(s.proj, 1)

                chunks(nc, pe, chunk)

            @block.sync
            def _(sp):
                def chunk(i):
                    sp.wait_ge(s.rows, i + 1)
                    sp.dma_start(table_rows(io.table2, i), rows[:, :, 0:D]).then_inc(s.stored, 16)
                    sp.dma_start(table_rows(io.xr_table, i), rows[:, :, D:2 * D]).then_inc(s.stored, 16)

                chunks(nc, sp, chunk)
                sp.wait_ge(s.stored, 32 * CH)
    phase_end(nc, s)


def ffn_phase(nc, io, sb):
    s = sems(nc, "ffn", "den", "inv", "attn", "plus_h", "back", "ln1_steps", "ln1_std", "t1", "t1_copied", "up", "gelu", "down",
             "biased", "resid", "ln2_steps", "ln2_std", "x_new", "ln3_steps", "ln3_std", "t3", "t3_copied", "proj", "rows",
             "stored")
    with ExitStack() as ctx:
        def tile(name, shape, dt=F32):
            return ctx.enter_context(nc.sbuf_tensor(f"ffn_{name}", shape, dt))[:]

        w = ln_work(tile, "ln")
        den = tile("den", [P, GE])
        attn = tile("attn", [P, GE])
        hh = tile("hh", [P, TPG, D])
        hhT = tile("hhT", [P, GE])
        gelu = tile("gelu", [P, 4, GE])
        res = tile("res", [P, TPG, D])
        out2 = tile("out2", [P, TPG, D])
        h = tile("h", [P, TPG, D])
        hs = tile("hs", [P, GE])
        rows = tile("rows", [P, TPG, D + 8])
        proj = sb.psum[:, 6:8, :].rearrange("p a (b f) -> p (a b) f", b=2)[:, :, 0:D + 8]
        with nc.Block() as block:
            @block.vector
            def _(v):
                def chunk(i):
                    x = sb.x[:, bass.ds(i * TPG, TPG), :]
                    freed(v, s.back, i)
                    v.tensor_scalar(den, sb.sums[:, 1, nodes_of(i)], 1e-16, None, ALU.add).then_inc(s.den, 1)
                    v.wait_ge(s.den, i + 1)
                    v.reciprocal(den, den).then_inc(s.inv, 1)
                    v.wait_ge(s.inv, i + 1)
                    v.tensor_tensor(den, den, sb.sums[:, 0, nodes_of(i)], ALU.mult).then_inc(s.attn, 1)
                    v.wait_ge(s.attn, i + 1)
                    v.scalar_tensor_tensor(attn, den, sb.L2_batt, sb.hT[:, nodes_of(i)], ALU.add, ALU.add).then_inc(s.plus_h, 1)
                    v.wait_ge(s.back, i + 1)
                    freed(v, s.t1, i)
                    freed(v, s.resid, i)
                    ln_vector(v, i, s.ln1_steps, s.ln1_std, sb.psum[:, 0, :].rearrange("p (b f) -> p b f", b=TPG), w, hh,
                              False, sb.L2_g1, sb.L2_be1)
                    v.wait_ge(s.down, i + 1)
                    v.tensor_tensor(res, sb.psum[:, 5, :].rearrange("p (b f) -> p b f", b=TPG),
                                    sb.L2_b2.unsqueeze(1).broadcast_to([P, TPG, D]), ALU.add).then_inc(s.biased, 1)
                    v.wait_ge(s.biased, i + 1)
                    v.tensor_tensor(res, res, hh, ALU.add).then_inc(s.resid, 1)
                    v.wait_ge(s.resid, i + 1)
                    ln_vector(v, i, s.ln2_steps, s.ln2_std, res, w, out2, False, sb.L2_g2, sb.L2_be2)
                    v.wait_ge(s.ln2_steps, i * (LN_STEPS + 2) + LN_STEPS + 2)
                    v.tensor_tensor(x, x, out2, ALU.add).then_inc(s.x_new, 1)
                    v.wait_ge(s.x_new, i + 1)
                    freed(v, s.t3, i)
                    settle(v)
                    ln_vector(v, i, s.ln3_steps, s.ln3_std, x, w, h, True)
                    v.wait_ge(s.proj, i + 1)
                    freed(v, s.stored, i * 32)
                    v.tensor_copy(rows, proj).then_inc(s.rows, 1)

                chunks(nc, v, chunk)

            @block.scalar
            def _(act):
                def chunk(i):
                    ln_scalar(act, i, s.ln1_steps, s.ln1_std, w, False)
                    act.wait_ge(s.t1, i + 1)
                    freed(act, s.up, i * 4)
                    act.activation(hhT, sb.psum[:, 0, :], ACT.Copy).then_inc(s.t1_copied, 1)
                    freed(act, s.down, i)
                    for q in range(4):
                        act.wait_ge(s.up, i * 4 + q + 1)
                        act.activation(gelu[:, q, :], sb.psum[:, 1 + q, :], ACT.Gelu, bias=sb.L2_b1[:, q:q + 1]).then_inc(s.gelu, 1)
                    ln_scalar(act, i, s.ln2_steps, s.ln2_std, w, False)
                    ln_scalar(act, i, s.ln3_steps, s.ln3_std, w, True)
                    act.wait_ge(s.t3, i + 1)
                    freed(act, s.proj, i)
                    act.activation(hs, sb.psum[:, 1, :], ACT.Copy).then_inc(s.t3_copied, 1)

                chunks(nc, act, chunk)

            @block.tensor
            def _(pe):
                def chunk(i):
                    pe.wait_ge(s.plus_h, i + 1)
                    freed(pe, s.t1_copied, i)
                    for b in range(TPG):
                        last = pe.transpose(sb.psum[:, 0, b * P:(b + 1) * P], attn[:, b * P:(b + 1) * P], sb.ident)
                    last.then_inc(s.back, 1)
                    pe.wait_ge(s.ln1_steps, i * (LN_STEPS + 2) + LN_STEPS + 2)
                    blocks_to_features(pe, sb.psum[:, 0, :], hh, sb.ident).then_inc(s.t1, 1)
                    pe.wait_ge(s.t1_copied, i + 1)
                    freed(pe, s.t3_copied, i)
                    freed(pe, s.gelu, i * 4)
                    for q in range(4):
                        pe.matmul(sb.psum[:, 1 + q, :], sb.L2_W1[:, q * P:(q + 1) * P], hhT, start=True, stop=True).then_inc(s.up, 1)
                    pe.wait_ge(s.gelu, i * 4 + 4)
                    freed(pe, s.biased, i)
                    for b in range(TPG):
                        for q in range(4):
                            last = pe.matmul(sb.psum[:, 5, b * P:(b + 1) * P], gelu[:, q, b * P:(b + 1) * P], sb.L2_W2[:, q, :],
                                             start=q == 0, stop=q == 3)
                    last.then_inc(s.down, 1)
                    pe.wait_ge(s.ln3_steps, i * LN_STEPS + 8)
                    blocks_to_features(pe, sb.psum[:, 1, :], h, sb.ident).then_inc(s.t3, 1)
                    pe.wait_ge(s.t3_copied, i + 1)
                    freed(pe, s.rows, i)
                    for b in range(TPG):
                        last = pe.matmul(proj[:, b, :], hs[:, b * P:(b + 1) * P], sb.L3_W1x, start=True, stop=True)
                    last.then_inc(s.proj, 1)

                chunks(nc, pe, chunk)

            @block.sync
            def _(sp):
                def chunk(i):
                    sp.wait_ge(s.rows, i + 1)
                    sp.dma_start(table_rows(io.table3, i), rows[:, :, 0:D + 4]).then_inc(s.stored, 16)
                    sp.dma_start(table_rows(io.adst3, i), rows[:, :, D + 4:D + 8]).then_inc(s.stored, 16)

                chunks(nc, sp, chunk)
                sp.wait_ge(s.stored, 32 * CH)
    phase_end(nc, s)


def gat_out_phase(nc, io, sb, last_layer):
    s = sems(nc, f"gat{1 + last_layer}", "den", "inv", "mean", "plus_b", "low", "exp", "elu", "proj", "rows", "stored")
    bias = sb.L3_b2 if last_layer else sb.L3_b1
    with ExitStack() as ctx:
        def tile(name, shape, dt=F32):
            return ctx.enter_context(nc.sbuf_tensor(f"gat{1 + last_layer}_{name}", shape, dt))[:]

        den = tile("den", [P, GE])
        v_in = tile("v_in", [P, GE])
        low = tile("low", [P, GE])
        ex = tile("ex", [P, GE])
        elu = tile("elu", [P, GE])
        rows = tile("rows", [P, TPG, D + 2])
        proj = sb.psum[:, 0:2, :].rearrange("p a (b f) -> p (a b) f", b=2)[:, :, 0:D + 2]
        with nc.Block() as block:
            @block.vector
            def _(v):
                def chunk(i):
                    freed(v, s.elu, i)
                    v.tensor_scalar(den, sb.sums[:, 1, nodes_of(i)], 1e-16, None, ALU.add).then_inc(s.den, 1)
                    v.wait_ge(s.den, i + 1)
                    v.reciprocal(den, den).then_inc(s.inv, 1)
                    v.wait_ge(s.inv, i + 1)
                    v.tensor_tensor(den, den, sb.sums[:, 0, nodes_of(i)], ALU.mult).then_inc(s.mean, 1)
                    v.wait_ge(s.mean, i + 1)
                    v.tensor_scalar(v_in, den, bias, None, ALU.add).then_inc(s.plus_b, 1)
                    v.wait_ge(s.plus_b, i + 1)
                    v.tensor_scalar(low, v_in, 0.0, None, ALU.min).then_inc(s.low, 1)
                    v.wait_ge(s.exp, i + 1)
                    v.tensor_scalar(ex, ex, -1.0, None, ALU.add).then_inc(s.low, 1)
                    v.wait_ge(s.low, i * 2 + 2)
                    freed(v, s.proj, i)
                    v.scalar_tensor_tensor(elu, v_in, 0.0, ex, ALU.max, ALU.add).then_inc(s.elu, 1)
                    v.wait_ge(s.proj, i + 1)
                    if last_layer:
                        x = sb.x[:, bass.ds(i * TPG, TPG), :]
                        v.tensor_tensor(x, x, proj[:, :, 0:D], ALU.add).then_inc(s.rows, 1)
                    else:
                        freed(v, s.stored, i * 32)
                        v.tensor_copy(rows, proj).then_inc(s.rows, 1)

                chunks(nc, v, chunk)

            @block.scalar
            def _(act):
                def chunk(i):
                    act.wait_ge(s.low, i * 2 + 1)
                    act.activation(ex, low, ACT.Exp).then_inc(s.exp, 1)

                chunks(nc, act, chunk)

            @block.tensor
            def _(pe):
                def chunk(i):
                    pe.wait_ge(s.elu, i + 1)
                    freed(pe, s.rows, i)
                    for b in range(TPG):
                        block_of = elu[:, b * P:(b + 1) * P]
                        if last_layer:
                            last = pe.transpose(proj[:, b, 0:D], block_of, sb.ident)
                        else:
                            last = pe.matmul(proj[:, b, :], block_of, sb.L3_W2x, start=True, stop=True)
                    last.then_inc(s.proj, 1)

                chunks(nc, pe, chunk)

            @block.sync
            def _(sp):
                if last_layer:
                    sp.wait_ge(s.rows, CH)
                    whole = N // P
                    sp.dma_start(io.out[0:whole * P, :].rearrange("(b p) f -> p b f", p=P), sb.x[:, 0:whole, :]).then_inc(s.stored, 16)
                    sp.dma_start(io.out[whole * P:N, :], sb.x[0:N - whole * P, whole, :]).then_inc(s.stored, 16)
                    sp.wait_ge(s.stored, 32)
                    return
                def chunk(i):
                    sp.wait_ge(s.rows, i + 1)
                    sp.dma_start(table_rows(io.table4, i), rows[:, :, 0:D + 1]).then_inc(s.stored, 16)
                    sp.dma_start(table_rows(io.adst4, i), rows[:, :, D:D + 2]).then_inc(s.stored, 16)

                chunks(nc, sp, chunk)
                sp.wait_ge(s.stored, 32 * CH)
    phase_end(nc, s)


def build(nc, io):
    def dram(name, shape):
        return nc.dram_tensor(name, shape, F32, kind="Internal").ap()

    io = named(
        **io,
        starts=dram("segment_starts", (1, EP + 1)),
        table0=dram("table0", (NP, D)), table1=dram("table1", (NP, D)),
        table2=dram("table2", (NP, D)), xr_table=dram("xr_table", (NP, D)),
        table3=dram("table3", (NP, D + 4)), adst3=dram("adst3", (NP, 4)),
        table4=dram("table4", (NP, D + 1)), adst4=dram("adst4", (NP, 2)),
    )
    with ExitStack() as ctx:
        def tile(name, shape, dt=F32):
            return ctx.enter_context(nc.sbuf_tensor(name, shape, dt))[:]

        sb = named(
            x=tile("x_nodes", [P, NP // P, D]), hT=tile("hT", [P, NP]), sums=tile("sums", [P, 2, NP]),
            ident=tile("ident", [P, P]), iota=tile("iota", [P, P]), mask8=tile("mask8", [P, 8]), mask4=tile("mask4", [P, 4]),
            expand8=tile("expand8", [8, P]), expand4=tile("expand4", [4, P]), ones_row=tile("ones_row", [1, P]),
            window_row=tile("window_row", [1, T], I32), rel=tile("rel", [P, T]),
            L0_We=tile("L0_We", [64, D]), L0_W1=tile("L0_W1", [P, D]), L0_W2=tile("L0_W2", [P, D]),
            L0_b1=tile("L0_b1", [P, 1]), L0_b2=tile("L0_b2", [P, 1]), L0_gamma=tile("L0_gamma", [P, 1]),
            L0_beta=tile("L0_beta", [P, 1]), L0_be=tile("L0_be", [P, D]), L0_eps=tile("L0_eps", [P, 1]),
            bn_scale=tile("bn_scale", [P, 1]), bn_shift=tile("bn_shift", [P, 1]),
            L1_W=tile("L1_W", [P, 2, D]), L1_b=tile("L1_b", [P, D]),
            L2_Wlr=tile("L2_Wlr", [P, 2 * D]), L2_blr=tile("L2_blr", [P, 2 * D]), L2_We=tile("L2_We", [P, D]),
            L2_att=tile("L2_att", [P, D]), L2_batt=tile("L2_batt", [P, 1]),
            L2_W1=tile("L2_W1", [P, 4 * D]), L2_b1=tile("L2_b1", [P, 4]), L2_W2=tile("L2_W2", [P, 4, D]),
            L2_b2=tile("L2_b2", [P, D]), L2_g1=tile("L2_g1", [P, D]), L2_be1=tile("L2_be1", [P, D]),
            L2_g2=tile("L2_g2", [P, D]), L2_be2=tile("L2_be2", [P, D]),
            L3_W1x=tile("L3_W1x", [P, D + 8]), L3_W2x=tile("L3_W2x", [P, D + 2]),
            L3_b1=tile("L3_b1", [P, 1]), L3_b2=tile("L3_b2", [P, 1]),
            psum=ctx.enter_context(nc.psum_tensor("psum", [P, 8, GE], F32))[:],
        )
        setup_phase(nc, io, sb)
        norm0_phase(nc, io, sb)
        edge_phase(nc, io, sb, 0)
        mlp0_phase(nc, io, sb)
        norm1_phase(nc, io, sb)
        edge_phase(nc, io, sb, 1)
        layer1_phase(nc, io, sb)
        edge_phase(nc, io, sb, 2)
        ffn_phase(nc, io, sb)
        edge_phase(nc, io, sb, 3)
        gat_out_phase(nc, io, sb, False)
        edge_phase(nc, io, sb, 4)
        gat_out_phase(nc, io, sb, True)


def laid_out(a):
    def pad_rows(x, n, value=0):
        out = np.full((n,) + x.shape[1:], value, x.dtype)
        out[:x.shape[0]] = x
        return out

    src = pad_rows(np.asarray(a["src"]), EP)
    dst = pad_rows(np.asarray(a["dst"]), EP, N)
    heads = {h: np.kron(np.eye(h, dtype=np.float32), np.ones((D // h, 1), np.float32)) for h in (4, 8)}
    col = lambda x: np.asarray(x).reshape(-1, 1)
    row = lambda x: np.asarray(x).reshape(-1)
    att = lambda n: np.stack([np.asarray(a[f"L3_gnn_att_src{n}"]).reshape(-1), np.asarray(a[f"L3_gnn_att_dst{n}"]).reshape(-1)], 1)
    return {
        "x": pad_rows(np.asarray(a["x"]), NP),
        "src_g": src.reshape(G, TPG, P).transpose(0, 2, 1),
        "dst_t": dst.reshape(T, P).T,
        "window": dst[::P].reshape(1, T),
        "dst_row": np.concatenate([np.full(1, -1, dst.dtype), dst]).reshape(1, EP + 1),
        "ea64T": pad_rows(np.asarray(a["edge_attr_64"]), EP).T,
        "ea128T": pad_rows(np.asarray(a["edge_attr_128"]), EP).T,
        "ident": np.eye(P, dtype=np.float32),
        "iota": np.tile(np.arange(P, dtype=np.float32), (P, 1)),
        "mask8": heads[8], "mask4": heads[4], "expand8": heads[8].T, "expand4": heads[4].T,
        "ones_row": np.ones((1, P), np.float32),
        "L0_We": a["L0_gnn_We"], "L0_W1": a["L0_gnn_W1"], "L0_W2": a["L0_gnn_W2"],
        "L0_b1": col(a["L0_gnn_b1"]), "L0_b2": col(a["L0_gnn_b2"]), "L0_gamma": col(a["L0_gnn_gamma"]),
        "L0_beta": col(a["L0_gnn_beta"]), "L0_be": row(a["L0_gnn_be"]), "L0_eps": row(a["L0_gnn_eps"]),
        "L1_WT": np.asarray(a["L1_gnn_W"]).T, "L1_b": row(a["L1_gnn_b"]),
        "L2_Wl": a["L2_gnn_W_l"], "L2_Wr": a["L2_gnn_W_r"], "L2_We": a["L2_gnn_W_e"],
        "L2_bl": row(a["L2_gnn_b_l"]), "L2_br": row(a["L2_gnn_b_r"]), "L2_att": row(a["L2_gnn_att"]),
        "L2_batt": col(a["L2_gnn_b_att"]), "L2_W1": a["L2_gnn_W1"], "L2_b1": np.asarray(a["L2_gnn_b1"]).reshape(4, P).T, "L2_W2": a["L2_gnn_W2"],
        "L2_b2": row(a["L2_gnn_b2"]), "L2_g1": row(a["L2_gnn_g1"]), "L2_be1": row(a["L2_gnn_be1"]),
        "L2_g2": row(a["L2_gnn_g2"]), "L2_be2": row(a["L2_gnn_be2"]),
        "L3_W1": a["L3_gnn_W1"], "L3_W1T": np.asarray(a["L3_gnn_W1"]).T, "L3_W2": a["L3_gnn_W2"],
        "L3_W2T": np.asarray(a["L3_gnn_W2"]).T, "L3_att1": att(1), "L3_att2": att(2),
        "L3_b1": col(a["L3_gnn_b1"]), "L3_b2": col(a["L3_gnn_b2"]),
    }


def kernel(**inputs):
    import concourse.bacc as bacc
    from concourse.bass_utils import run_bass_kernel_spmd

    nc = bacc.Bacc("TRN2", target_bir_lowering=False, num_devices=1)
    arrays, io = {}, {}
    for name, value in laid_out(inputs).items():
        value = np.ascontiguousarray(value)
        arrays[f"in_{name}"] = value
        io[name] = nc.dram_tensor(f"in_{name}", value.shape, mybir.dt.from_np(value.dtype), kind="ExternalInput").ap()
    io["out"] = nc.dram_tensor("out_0", (N, D), F32, kind="ExternalOutput").ap()
    build(nc, io)
    result = run_bass_kernel_spmd(nc, [arrays], core_ids=[0])
    return result.results[0]["out_0"]
```

```python
from collections import namedtuple
from contextlib import ExitStack

import concourse.bass as bass
import concourse.mybir as mybir
import numpy as np

F32 = mybir.dt.float32
I32 = mybir.dt.int32
ALU = mybir.AluOpType
ACT = mybir.ActivationFunctionType
AX = mybir.AxisListType.X
DVE = mybir.EngineType.DVE
SP = mybir.EngineType.SP

P = 128
D = 128
N = 6250
E = 106250
TPG = 4
GE = TPG * P
UNROLL = 8
G = -(-E // (GE * UNROLL)) * UNROLL
T = G * TPG
EP = G * GE
CH = -(-(N + P) // GE)
NP = CH * GE
NARROW = 64
NEG = -3.0e38
LN_EPS = 1e-5
BOUND = "destinations are node numbers, so a window starts at a column of the aggregate"


def named(**things):
    return namedtuple("Named", things)(**things)


def sems(nc, phase, *names, **slots):
    lists = {n: [nc.alloc_semaphore(f"{phase}_{n}{k}") for k in range(count)] for n, count in slots.items()}
    return named(**{n: nc.alloc_semaphore(f"{phase}_{n}") for n in names}, **lists)


def phase_end(nc, s):
    nc.clear_and_free_semaphores([h for v in s for h in (v if isinstance(v, list) else [v])])
    nc.all_engine_barrier()


def settle(eng):
    eng.nop(nofuse=True)


class At:

    def __init__(self, i, base, unroll=UNROLL):
        self.i, self.base, self.unroll = i, base, unroll

    def back(self, k):
        return At(self.i, self.base - k, self.unroll)

    def times(self, n, add=0):
        c = n * self.base + add
        return c if self.i is None else self.i * (n * self.unroll) + c

    def uses(self, slots, n=1):
        c = n * (self.base // slots + 1)
        return c if self.i is None else self.i * (n * (self.unroll // slots)) + c

    def nth(self, j=1, n=1):
        c = n * (self.base // 2) + j
        return c if self.i is None else self.i * n + c

    def slot(self, slots):
        return self.base % slots

    def exists(self):
        return self.i is not None or 0 <= self.base < G


def within(nc, i, low, high):
    return nc.s_assert_within(i, low, high, skip_runtime_bounds_check_because="the loop's own bounds")


def sweep(nc, eng, first, steady, steady_end, last, emit):
    rounds = (steady_end + 1 - steady) // UNROLL
    for s in range(first, steady):
        emit(At(None, s))
    with eng.Fori(0, rounds) as i:
        i = within(nc, i, 0, rounds - 1)
        for j in range(UNROLL):
            emit(At(i, steady + j))
    for s in range(steady + rounds * UNROLL, last + 1):
        emit(At(None, s))


def chunks(nc, eng, stages):
    def together(*pair):
        for stage in stages:
            for c in pair:
                stage(c)

    together(At(None, 0, 2))
    together(At(None, 1, 2), At(None, 2, 2))
    rounds = (CH - 3) // 2
    with eng.Fori(0, rounds) as i:
        i = within(nc, i, 0, rounds - 1)
        together(At(i, 3, 2), At(i, 4, 2))


def skewed(nc, eng, parts, stages):
    order = sorted(stages, key=lambda stage: (stage[1], -stage[0]))

    def together(c):
        for part, _, stage in order:
            if c.i is not None or 0 <= c.base - part < CH:
                stage(c.back(part))

    first = parts + 1
    rounds = (CH - first) // 2
    for n in range(first):
        together(At(None, n, 2))
    with eng.Fori(0, rounds) as i:
        i = within(nc, i, 0, rounds - 1)
        together(At(i, first, 2))
        together(At(i, first + 1, 2))
    for n in range(first + 2 * rounds, CH + parts - 1):
        together(At(None, n, 2))


def wait_past(eng, sem, at, n, add):
    v = at.times(n, add)
    if at.i is not None or v > 0:
        eng.wait_ge(sem, v)


def freed(eng, sem, c, n=1):
    if c.i is not None or c.base >= 2:
        eng.wait_ge(sem[c.slot(2)], c.nth(0, n))


def passed(eng, sem, c, n=1):
    b = c.back(1)
    if b.i is not None or b.base >= 0:
        eng.wait_ge(sem[b.slot(2)], b.nth(n, n))


def setup_phase(nc, io, sb):
    s = sems(nc, "setup", "loaded", "prep_loaded", "relative", "starts", "starts_stored", "masked", "folded", "fold_copied",
             "widest", "widest_T", "narrow")
    loads = [
        (sb.x, io.x.rearrange("(b p) f -> p b f", p=P)),
        (sb.ident, io.ident), (sb.iota, io.iota), (sb.mask4, io.mask4),
        (sb.expand8, io.expand8), (sb.expand4, io.expand4), (sb.ones_row, io.ones_row),
        (sb.window_row, io.window),
        (sb.L0_We, io.L0_We), (sb.L0_W1, io.L0_W1), (sb.L0_W2, io.L0_W2),
        (sb.L0_b1, io.L0_b1), (sb.L0_b2, io.L0_b2), (sb.L0_gamma, io.L0_gamma), (sb.L0_beta, io.L0_beta),
        (sb.L0_be, io.L0_be.partition_broadcast(P)),
        (sb.L0_eps, io.L0_eps.partition_broadcast(P)),
        (sb.L1_W[:, 0, :], io.L1_WT[0:D]), (sb.L1_W[:, 1, :], io.L1_WT[D:2 * D]),
        (sb.L1_b, io.L1_b),
        (sb.L2_Wlr[:, 0:D], io.L2_Wl), (sb.L2_Wlr[:, D:2 * D], io.L2_Wr), (sb.L2_We, io.L2_We),
        (sb.L2_blr[:, 0:D], io.L2_bl.partition_broadcast(P)), (sb.L2_blr[:, D:2 * D], io.L2_br.partition_broadcast(P)),
        (sb.L2_att, io.L2_att.partition_broadcast(P)), (sb.L2_batt, io.L2_batt),
        (sb.L2_W1, io.L2_W1), (sb.L2_b1, io.L2_b1),
        (sb.L2_W2, io.L2_W2.rearrange("(q p) f -> p q f", p=P)), (sb.L2_b2, io.L2_b2),
        (sb.L2_g1, io.L2_g1.partition_broadcast(P)), (sb.L2_be1, io.L2_be1.partition_broadcast(P)),
        (sb.L2_g2, io.L2_g2.partition_broadcast(P)), (sb.L2_be2, io.L2_be2.partition_broadcast(P)),
        (sb.L3_W1x[:, 0:D], io.L3_W1), (sb.L3_W2x[:, 0:D], io.L3_W2),
        (sb.L3_b1, io.L3_b1.partition_broadcast(P)), (sb.L3_b2, io.L3_b2.partition_broadcast(P)),
    ]
    with ExitStack() as ctx:
        def tile(name, shape, dt=F32):
            return ctx.enter_context(nc.sbuf_tensor(f"setup_{name}", shape, dt))[:]

        dst_of = tile("dst_of", [P, T], I32)
        window_all = tile("window_all", [P, T], I32)
        here = tile("here", [P, T], I32)
        before = tile("before", [P, T], I32)
        starts = tile("starts", [P, T])
        tail = tile("tail", [1, 1])
        w1t = tile("w1t", [P, D])
        w2t = tile("w2t", [P, D])
        att1 = tile("att1", [P, 2])
        att2 = tile("att2", [P, 2])
        fold1 = tile("fold1", [P, 8])
        widest = tile("widest", [P, 1])
        widest_all = tile("widest_all", [1, 1])
        psum = sb.psum
        with nc.Block() as block:
            @block.sync
            def _(sp):
                sp.dma_start(dst_of, io.dst_t).then_inc(s.prep_loaded, 16)
                sp.dma_start(window_all, io.window.partition_broadcast(P)).then_inc(s.prep_loaded, 16)
                sp.dma_start(here, io.dst_row[0:1, 1:EP + 1].rearrange("a (p t) -> (a p) t", p=P)).then_inc(s.prep_loaded, 16)
                sp.dma_start(before, io.dst_row[0:1, 0:EP].rearrange("a (p t) -> (a p) t", p=P)).then_inc(s.prep_loaded, 16)
                sp.dma_start(w1t, io.L3_W1T).then_inc(s.prep_loaded, 16)
                sp.dma_start(w2t, io.L3_W2T).then_inc(s.prep_loaded, 16)
                sp.dma_start(att1, io.L3_att1).then_inc(s.prep_loaded, 16)
                sp.dma_start(att2, io.L3_att2).then_inc(s.prep_loaded, 16)
                for to, of in loads:
                    sp.dma_start(to, of).then_inc(s.loaded, 16)
                sp.wait_ge(s.starts, 2)
                sp.dma_start(io.starts[0:1, 0:EP].rearrange("a (p t) -> (a p) t", p=P), starts).then_inc(s.starts_stored, 16)
                sp.dma_start(io.starts[0:1, EP:EP + 1], tail).then_inc(s.starts_stored, 16)
                sp.wait_ge(s.starts_stored, 32)
                sp.wait_ge(s.loaded, 16 * len(loads))

            @block.vector
            def _(v):
                v.memset(tail, NEG).then_inc(s.starts, 1)
                v.wait_ge(s.prep_loaded, 16 * 8)
                v.tensor_tensor(sb.rel_tile, dst_of, window_all, ALU.subtract).then_inc(s.relative, 1)
                v.tensor_tensor(sb.rel_group.rearrange("p (g t) -> p g t", t=TPG), dst_of.rearrange("p (g t) -> p g t", t=TPG),
                                window_all[:, 0:T:TPG].unsqueeze(2).broadcast_to([P, G, TPG]), ALU.subtract).then_inc(s.relative, 1)
                v.tensor_tensor(starts, here, before, ALU.not_equal).then_inc(s.relative, 1)
                v.wait_ge(s.relative, 3)
                v.tensor_scalar(starts, starts, NEG, None, ALU.mult).then_inc(s.starts, 1)
                v.tensor_reduce(widest, sb.rel_group, AX, ALU.max).then_inc(s.widest, 1)
                v.wait_ge(s.loaded, 16 * len(loads))
                v.tensor_scalar(fold1[:, 0:4], sb.mask4, att1[:, 0:1], None, ALU.mult).then_inc(s.masked, 1)
                v.tensor_scalar(fold1[:, 4:8], sb.mask4, att1[:, 1:2], None, ALU.mult).then_inc(s.masked, 1)
                v.wait_ge(s.folded, 1)
                v.tensor_copy(sb.L3_W1x[:, D:D + 8], psum[:, 0, 0:8]).then_inc(s.fold_copied, 1)
                v.tensor_copy(sb.L3_W2x[:, D:D + 2], psum[:, 1, 0:2]).then_inc(s.fold_copied, 1)
                v.wait_ge(s.widest_T, 1)
                v.tensor_reduce(widest_all, psum[0:1, 2, 0:P], AX, ALU.max).then_inc(s.narrow, 1)
                v.wait_ge(s.narrow, 1)
                v.tensor_scalar(sb.narrow, widest_all, float(NARROW), None, ALU.is_lt).then_inc(s.narrow, 1)

            @block.tensor
            def _(pe):
                pe.wait_ge(s.prep_loaded, 16 * 8)
                pe.wait_ge(s.masked, 2)
                pe.matmul(psum[:, 0, 0:8], w1t, fold1, start=True, stop=True)
                pe.matmul(psum[:, 1, 0:2], w2t, att2, start=True, stop=True).then_inc(s.folded, 1)
                pe.wait_ge(s.loaded, 16 * len(loads))
                pe.wait_ge(s.widest, 1)
                pe.transpose(psum[0:1, 2, 0:P], widest, sb.ident).then_inc(s.widest_T, 1)
    phase_end(nc, s)


LN_N = 2 * TPG + 3


class LayerNorm:

    def __init__(self, tile, name, ln, root):
        self.ln, self.root = ln, root
        self.stats = tile(name + "_stats", [P, 2, TPG, 6])
        self.mean_var = tile(name + "_mean_var", [P, 2, TPG, 2])
        self.std = tile(name + "_std", [P, 2, TPG])
        self.rstd = tile(name + "_rstd", [P, 2, TPG])
        self.shift = tile(name + "_shift", [P, 2, TPG])

    def statistics(self, v, c, x, applied):
        k, ln = c.slot(2), self.ln[c.slot(2)]
        freed(v, applied, c)
        settle(v)
        for b in range(TPG):
            v.bn_stats(self.stats[:, k, b, :], x[:, b, :]).then_inc(ln, 1)
        v.wait_ge(ln, c.nth(TPG, LN_N))
        settle(v)
        for b in range(TPG):
            v.bn_aggr(self.mean_var[:, k, b, :], self.stats[:, k, b, :]).then_inc(ln, 1)
        v.wait_ge(ln, c.nth(2 * TPG, LN_N))
        var = self.mean_var[:, k, :, 1]
        v.tensor_scalar(var, var, LN_EPS, None, ALU.add).then_inc(ln, 1)

    def take_root(self, act, c):
        k = c.slot(2)
        act.wait_ge(self.ln[k], c.nth(2 * TPG + 1, LN_N))
        act.activation(self.std[:, k], self.mean_var[:, k, :, 1], ACT.Sqrt).then_inc(self.root[k], 1)

    def scale_shift(self, v, c):
        k, ln = c.slot(2), self.ln[c.slot(2)]
        v.wait_ge(self.root[k], c.nth())
        v.reciprocal(self.rstd[:, k], self.std[:, k]).then_inc(ln, 1)
        v.wait_ge(ln, c.nth(2 * TPG + 2, LN_N))
        v.scalar_tensor_tensor(self.shift[:, k], self.mean_var[:, k, :, 0], -1.0, self.rstd[:, k], ALU.mult, ALU.mult).then_inc(ln, 1)

    def apply(self, act, c, out, x, function, done):
        k = c.slot(2)
        act.wait_ge(self.ln[k], c.nth(LN_N, LN_N))
        for b in range(TPG):
            last = act.activation(out[:, b, :], x[:, b, :], function, bias=self.shift[:, k, b:b + 1], scale=self.rstd[:, k, b:b + 1])
        last.then_inc(done[k], 1)


def nodes_of(c):
    return bass.ds(c.times(GE), GE)


def blocks_of(sb, c):
    return sb.x[:, bass.ds(c.times(TPG), TPG), :]


def table_rows(table, c):
    return table[nodes_of(c), :].rearrange("(b p) f -> p b f", p=P)


def flip(pe, out, source, ident, rows=P):
    for b in range(TPG):
        last = pe.transpose(out(b), source(b), ident[0:rows, 0:rows])
    return last


def piece(b):
    return slice(b * P, (b + 1) * P)


def node_phase(nc, name, ctx):
    def tile(part, shape, dt=F32):
        return ctx.enter_context(nc.sbuf_tensor(f"{name}_{part}", shape, dt))[:]

    return tile


def norm0_phase(nc, io, sb):
    s = sems(nc, "norm0", ln=2, root=2, h=2, transposed=2, kept=2, rows=2, stored=2)
    with ExitStack() as ctx:
        tile = node_phase(nc, "norm0", ctx)
        norm = LayerNorm(tile, "ln", s.ln, s.root)
        h = tile("h", [P, 2, TPG, D])
        rows = tile("rows", [P, 2, TPG, D])
        bank = [sb.psum[:, k, :] for k in range(2)]
        with nc.Block() as block:
            @block.vector
            def _(v):
                def rows_out(c):
                    k = c.slot(2)
                    v.wait_ge(s.h[k], c.nth())
                    freed(v, s.stored, c, 16)
                    v.tensor_tensor(rows[:, k], h[:, k], sb.L0_be.unsqueeze(1).broadcast_to([P, TPG, D]), ALU.add).then_inc(s.rows[k], 1)

                chunks(nc, v, [lambda c: norm.statistics(v, c, blocks_of(sb, c), s.h), lambda c: norm.scale_shift(v, c), rows_out])

            @block.scalar
            def _(act):
                def normalise(c):
                    freed(act, s.transposed, c)
                    freed(act, s.rows, c)
                    norm.apply(act, c, h[:, c.slot(2)], blocks_of(sb, c), ACT.Relu, s.h)

                def keep(c):
                    k = c.slot(2)
                    act.wait_ge(s.transposed[k], c.nth())
                    act.activation(sb.hT[:, nodes_of(c)], bank[k], ACT.Copy).then_inc(s.kept[k], 1)

                chunks(nc, act, [lambda c: norm.take_root(act, c), normalise, keep])

            @block.tensor
            def _(pe):
                def transpose(c):
                    k = c.slot(2)
                    pe.wait_ge(s.h[k], c.nth())
                    freed(pe, s.kept, c)
                    flip(pe, lambda b: bank[k][:, piece(b)], lambda b: h[:, k, b, :], sb.ident).then_inc(s.transposed[k], 1)

                chunks(nc, pe, [transpose])

            @block.sync
            def _(sp):
                def store(c):
                    k = c.slot(2)
                    sp.wait_ge(s.rows[k], c.nth())
                    sp.dma_start(table_rows(io.table0, c), rows[:, k]).then_inc(s.stored[k], 16)

                chunks(nc, sp, [store])
                sp.wait_ge(s.stored[0], 16 * (CH - CH // 2))
                sp.wait_ge(s.stored[1], 16 * (CH // 2))
    phase_end(nc, s)


def edge_phase(nc, io, sb, layer):
    narrow = nc.values_load(sb.narrow, min_val=0, max_val=1)
    with nc.If(narrow > 0):
        edge_sweep(nc, io, sb, layer, True)
    with nc.Else():
        edge_sweep(nc, io, sb, layer, False)


def edge_sweep(nc, io, sb, layer, narrow):
    W, WINDOWS = (NARROW, 1) if narrow else (P, TPG)
    rel = sb.rel_group if narrow else sb.rel_tile
    AHEAD = 4 if narrow else 2
    H = {0: 0, 1: 1, 2: 8, 3: 4, 4: 1}[layer]
    soft = layer >= 2
    attr = {0: io.ea64T, 2: io.ea128T}.get(layer)
    table, width = {0: (io.table0, D), 1: (io.table1, D + 1), 2: (io.table2, D),
                    3: (io.table3, D + 4), 4: (io.table4, D + 1)}[layer]
    dst_table, dst_width = {2: (io.xr_table, D), 3: (io.adst3, 4), 4: (io.adst4, 2)}.get(layer, (None, 0))
    expand = {2: sb.expand8, 3: sb.expand4, 4: sb.ones_row}.get(layer)
    TERM = D if layer in (0, 2) else H
    phase = f"edges{layer}{'n' if narrow else 'w'}"
    names = "onehot distance edge_term term_read relued scattered window_copied window_T order".split()
    if soft:
        names += ("onehotT_psum onehotT leaky logits logits_lane running lanes maxima_psum factor_log factor "
                  "factor_psum factor_copied shifted weights message").split()
    s = sems(nc, phase, *names, indices=8, gathered=8, attr=AHEAD, dst_rows=AHEAD, starts=AHEAD)
    rows_read = s.message if soft else s.term_read if layer == 0 else s.scattered

    with ExitStack() as ctx:
        def tile(name, shape, dt=F32):
            return ctx.enter_context(nc.sbuf_tensor(f"{phase}_{name}", shape, dt))[:]

        idx = tile("idx", [P, 8, TPG], I32)
        rows = tile("rows", [P, 8, TPG, width])
        onehot = tile("onehot", [P, 8, TPG, W])
        window = tile("window", [W, WINDOWS, D + H])
        if attr is not None:
            attrs = tile("attrs", [attr.shape[0], AHEAD, GE])
            term = tile("term", [P, 2, TPG, D])
        if layer != 1:
            message = tile("message", [P, 2, TPG, D + H])
        if layer == 2:
            distance = tile("distance", [P, TPG, W])
            one = tile("one", [P, 1])
            growth = tile("growth", [H, 2])
            relued = tile("relued", [P, 2, TPG, D])
        if soft:
            onehotT = tile("onehotT", [W, 2, GE])
            dst_rows = tile("dst_rows", [W, AHEAD, WINDOWS, dst_width])
            starts = tile("seg_starts", [H, AHEAD, GE + 1])
            linear = tile("linear", [P, TPG, H])
            logits = tile("logits", [P, 2, TPG, H])
            running = tile("running", [H, 2, GE])
            maxima = tile("maxima", [H, 2, GE])
            factor_log = tile("factor_log", [H, 2])
            factor = tile("factor", [H, 4])
            factor_of = tile("factor_of", [P, 4])
            shifted = tile("shifted", [P, 2, TPG, H])
        TERMS = 2 if narrow else 1
        term_bank = [sb.psum[:, k % TERMS, :] for k in range(2)]
        onehotT_bank = sb.psum[0:W, 2, :]
        lane_bank = sb.psum[:, 3, :]
        window_bank = sb.psum[0:W, 4:6, :].rearrange("p a (t n) -> p (a t) n", t=2)[:, 0:WINDOWS, 0:D + H]
        maxima_bank = sb.psum[:, 5 if narrow else 1, 0:TPG * H]
        factor_bank = sb.psum[:, 5 if narrow else 1, TPG * H:TPG * H + 1]
        window_T = sb.psum[:, 6:8, :].rearrange("p a (t n) -> p (a t) n", t=2)
        HEADS = H > 0
        ORDER = (1 + HEADS) * WINDOWS + 2 * soft
        FIRST = 1 + HEADS + soft + (layer == 2)

        with nc.Block() as block:
            @block.sync
            def _(sp):
                def load(g):
                    k = g.slot(8)
                    if g.base >= 8:
                        sp.wait_ge(s.gathered[k], g.back(8).uses(8, 16 * TPG))
                    sp.dma_start(idx[:, k, :], io.src_g[bass.ds(g.times(1), 1)].rearrange("a p t -> (a p) t")).then_inc(s.indices[k], 16)
                    if layer != 1:
                        wait_past(sp, s.edge_term, g, 1, 1 - AHEAD)
                    if attr is not None:
                        sp.dma_start(attrs[:, g.slot(AHEAD), :], attr[:, bass.ds(g.times(GE), GE)]).then_inc(s.attr[g.slot(AHEAD)], 16)
                    if soft:
                        _, at = nc.values_load_multi_w_load_instructions(
                            sb.window_row[0:1, bass.ds(g.times(TPG), WINDOWS)], engines=[SP], min_val=0, max_val=N,
                            skip_runtime_bounds_check_because=BOUND)
                        for t in range(WINDOWS):
                            sp.dma_start(dst_rows[:, g.slot(AHEAD), t, :], dst_table[bass.ds(at[t], W), :]).then_inc(s.dst_rows[g.slot(AHEAD)], 16)
                        wait_past(sp, s.lanes, g, 1, 1 - AHEAD)
                        sp.dma_start(starts[:, g.slot(AHEAD), :],
                                     io.starts[0:1, bass.ds(g.times(GE), GE + 1)].rearrange("a n -> (a n)").partition_broadcast(H)).then_inc(s.starts[g.slot(AHEAD)], 16)

                sweep(nc, sp, 0, 8, G - 1, G - 1, load)

            @block.gpsimd
            def _(pool):
                def gather(g):
                    k = g.slot(8)
                    if g.base >= 8:
                        pool.wait_ge(rows_read, g.times(1, -7))
                    pool.wait_ge(s.indices[k], g.uses(8, 16))
                    settle(pool)
                    for t in range(TPG):
                        pool.indirect_dma_start(rows[:, k, t, :], None, table,
                                                bass.IndirectOffsetOnAxis(idx[:, k, t:t + 1], 0)).then_inc(s.gathered[k], 16)

                sweep(nc, pool, 0, 8, G - 1, G - 1, gather)

            @block.scalar
            def _(act):
                def step(t):
                    g = t
                    if g.exists() and soft:
                        act.wait_ge(s.onehotT_psum, g.times(1, 1))
                        wait_past(act, s.edge_term, g, 1, -1)
                        act.activation(onehotT[:, g.slot(2)], onehotT_bank, ACT.Copy).then_inc(s.onehotT, 1)
                    g = t.back(3)
                    if g.exists() and soft:
                        act.wait_ge(s.shifted, g.times(1, 1))
                        wait_past(act, s.scattered, g, 1, -1)
                        act.activation(message[:, g.slot(2), :, D:D + H], shifted[:, g.slot(2)], ACT.Exp).then_inc(s.weights, 1)
                    g = t.back(4)
                    if g.exists():
                        act.wait_ge(s.scattered, g.times(1, 1))
                        wait_past(act, s.window_T, g, 1, 0)
                        act.activation(window, window_bank, ACT.Copy).then_inc(s.window_copied, 1)
                    g = t.back(1)
                    if g.exists() and layer == 0:
                        act.wait_ge(s.term_read, g.times(1, 1))
                        wait_past(act, s.scattered, g, 1, -1)
                        act.activation(message[:, g.slot(2)], term[:, g.slot(2)], ACT.Relu).then_inc(s.relued, 1)
                    g = t.back(3)
                    if g.exists() and layer == 2:
                        act.wait_ge(s.factor_psum, g.times(1, 1))
                        act.wait_ge(s.shifted, g.times(1, 1))
                        wait_past(act, s.order, g, ORDER, FIRST - 3 * ORDER)
                        act.activation(factor_of[:, g.slot(4):g.slot(4) + 1], factor_bank, ACT.Copy).then_inc(s.factor_copied, 1)
                    g = At(t.i, t.base + 1)
                    if g.exists() and layer == 2:
                        if g.base == 0:
                            act.wait_ge(s.order, FIRST)
                        wait_past(act, s.onehot, g, 1, 0)
                        wait_past(act, s.scattered, g, 1, -7)
                        settle(act)
                        for k in range(TPG):
                            last = act.activation(distance[:, k, :], sb.iota[:, 0:W], ACT.Square, scale=-1.0,
                                                  bias=rel[:, bass.ds(g.times(TPG, k), 1)])
                        last.then_inc(s.distance, 1)
                        act.wait_ge(s.distance, g.times(1, 1))
                        act.activation(onehot[:, g.slot(8)], distance, ACT.Relu, scale=-1.0, bias=one).then_inc(s.onehot, 1)
                    g = t.back(2)
                    if g.exists() and layer == 2:
                        act.wait_ge(s.lanes, g.times(1, 1))
                        wait_past(act, s.factor, g, 1, -1)
                        act.activation(growth[:, g.slot(2):g.slot(2) + 1], running[:, 1 - g.slot(2), GE - 1:GE], ACT.Relu,
                                       scale=-1.0, bias=maxima[:, g.slot(2), 0:1]).then_inc(s.factor_log, 1)
                    if g.exists() and soft:
                        act.wait_ge(s.factor_log, g.times(1, 1))
                        wait_past(act, s.order, g, ORDER, FIRST - 3 * ORDER)
                        act.activation(factor[:, g.slot(4):g.slot(4) + 1], (growth if layer == 2 else factor_log)[:, g.slot(2):g.slot(2) + 1], ACT.Exp,
                                       scale=-1.0 if layer == 2 else 1.0).then_inc(s.factor, 1)
                    g = t
                    if g.exists() and layer == 2:
                        act.wait_ge(s.edge_term, g.times(1, 1))
                        wait_past(act, s.term_read, g, 1, -1)
                        act.activation(relued[:, g.slot(2)].rearrange("p t n -> p (t n)"), term_bank[g.slot(2)], ACT.Relu, scale=0.8).then_inc(s.relued, 1)

                sweep(nc, act, -1, 7, G - 2, G + 3, step)

            @block.tensor
            def _(pe):
                def step(t):
                    g = t.back(2)
                    if g.exists() and soft:
                        pe.wait_ge(s.logits, g.times(1, 1))
                        wait_past(pe, s.running, g, 1, 0)
                        for k in range(TPG):
                            last = pe.transpose(lane_bank[0:H, piece(k)], logits[:, g.slot(2), k, :], sb.ident)
                        last.then_inc(s.logits_lane, 1)
                    g = t
                    if g.exists() and soft:
                        pe.wait_ge(s.onehot, g.times(1, 1))
                        wait_past(pe, s.onehotT, g, 1, 0)
                        settle(pe)
                        for k in range(TPG):
                            last = pe.transpose(onehotT_bank[:, piece(k)], onehot[:, g.slot(8), k], sb.ident)
                        last.then_inc(s.onehotT_psum, 1)
                    g = t.back(4)
                    if g.exists():
                        wait_past(pe, s.window_copied, g, 1, 0)
                        pe.wait_ge(s.onehot, g.times(1, 1))
                        if soft:
                            pe.wait_ge(s.message, g.times(1, 1))
                        elif layer == 0:
                            pe.wait_ge(s.relued, g.times(1, 1))
                        else:
                            pe.wait_ge(s.gathered[g.slot(8)], g.uses(8, 16 * TPG))
                        for k in range(TPG):
                            what = rows[:, g.slot(8), k, :] if layer == 1 else message[:, g.slot(2), k, :]
                            last = pe.matmul(window_bank[:, 0 if narrow else k, :], onehot[:, g.slot(8), k], what,
                                             start=not narrow or k == 0, stop=not narrow or k == TPG - 1)
                        last.then_inc(s.scattered, 1)
                    g = t
                    if g.exists() and layer != 1:
                        wait_past(pe, s.term_read, g, 1, 1 - TERMS)
                        if attr is not None:
                            pe.wait_ge(s.attr[g.slot(AHEAD)], g.uses(AHEAD, 16))
                        if layer == 2:
                            pe.wait_ge(s.gathered[g.slot(8)], g.uses(8, 16 * TPG))
                        if soft:
                            pe.wait_ge(s.dst_rows[g.slot(AHEAD)], g.uses(AHEAD, 16 * WINDOWS))
                            pe.wait_ge(s.onehotT, g.times(1, 1))
                        for k in range(TPG):
                            out = term_bank[g.slot(2)][:, k * TERM:(k + 1) * TERM]
                            if attr is not None:
                                last = pe.matmul(out, attrs[:, g.slot(AHEAD), piece(k)], sb.L0_We if layer == 0 else sb.L2_We,
                                                 start=True, stop=not soft)
                            if layer == 2:
                                pe.matmul(out, sb.ident, rows[:, g.slot(8), k, :], start=False, stop=False)
                            if soft:
                                last = pe.matmul(out, onehotT[:, g.slot(2), piece(k)],
                                                 dst_rows[:, g.slot(AHEAD), 0 if narrow else k, dst_width - TERM:dst_width],
                                                 start=attr is None, stop=True)
                        last.then_inc(s.edge_term, 1)
                    g = t.back(4)
                    if g.exists():
                        pe.wait_ge(s.window_copied, g.times(1, 1))
                        wait_past(pe, s.order, g, ORDER, FIRST)
                        settle(pe)
                        for k in range(WINDOWS):
                            last = pe.transpose(window_T[:, k, 0:W], window[:, k, 0:D], sb.ident[0:W, 0:W])
                            if HEADS:
                                last = pe.transpose(window_T[0:H, k, P:P + W], window[:, k, D:D + H], sb.ident[0:W, 0:W])
                        last.then_inc(s.window_T, 1)
                    g = t.back(2)
                    if g.exists() and soft:
                        pe.wait_ge(s.lanes, g.times(1, 1))
                        wait_past(pe, s.factor_copied, g, 1, 0)
                        settle(pe)
                        for k in range(TPG):
                            last = pe.transpose(maxima_bank[:, k * H:(k + 1) * H], maxima[:, g.slot(2), piece(k)], sb.ident[0:H, 0:H])
                        last.then_inc(s.maxima_psum, 1)
                    g = t.back(2)
                    if g.exists() and soft:
                        pe.wait_ge(s.factor, g.times(1, 1))
                        settle(pe)
                        pe.matmul(factor_bank, expand, factor[:, g.slot(4):g.slot(4) + 1], start=True, stop=True).then_inc(s.factor_psum, 1)

                sweep(nc, pe, -1, 7, G - 2, G + 3, step)

            @block.vector
            def _(v):
                v.memset(sb.sums, 0.0).then_inc(s.order, 1)
                if HEADS:
                    v.memset(sb.weight_sums[0:H], 0.0).then_inc(s.order, 1)
                if soft:
                    v.memset(running[:, 1, :], NEG).then_inc(s.order, 1)
                if layer == 2:
                    v.memset(one, 1.0).then_inc(s.order, 1)
                v.wait_ge(s.order, FIRST)

                loaded = {}

                def columns(t, g):
                    body = narrow and t.i is not None
                    if body and t.base > 7:
                        return loaded[t.base]
                    row = sb.window_row[0:1, bass.ds(g.times(TPG), UNROLL * TPG)].rearrange("a (g t) -> a g t", t=TPG)[:, :, 0] if body \
                        else sb.window_row[0:1, bass.ds(g.times(TPG), WINDOWS)]
                    _, at = nc.values_load_multi_w_load_instructions(row, engines=[DVE], min_val=0, max_val=N,
                                                                     skip_runtime_bounds_check_because=BOUND)
                    if body:
                        for k in range(UNROLL):
                            loaded[t.base + k] = at[k:k + 1]
                    return at

                def step(t):
                    g = t.back(5)
                    if g.exists():
                        at = columns(t, g)
                        kinds = 1 + HEADS
                        j = 0
                        if soft:
                            v.wait_ge(s.factor_copied, g.times(1, 1))
                            for column, by in ((sb.sums[:, bass.ds(at[0], 1)], factor_of[:, g.slot(4):g.slot(4) + 1]),
                                               (sb.weight_sums[0:H, bass.ds(at[0], 1)], factor[:, g.slot(4):g.slot(4) + 1])):
                                wait_past(v, s.order, g, ORDER, FIRST + j - kinds + 1)
                                v.tensor_scalar(column, column, by, None, ALU.mult).then_inc(s.order, 1)
                                j += 1
                        v.wait_ge(s.window_T, g.times(1, 1))
                        for k in range(WINDOWS):
                            pairs = [(sb.sums[:, bass.ds(at[k], W)], window_T[:, k, 0:W])]
                            if HEADS:
                                pairs.append((sb.weight_sums[0:H, bass.ds(at[k], W)], window_T[0:H, k, P:P + W]))
                            for to, of in pairs:
                                wait_past(v, s.order, g, ORDER, FIRST + j - kinds + 1)
                                v.tensor_tensor(to, to, of, ALU.add).then_inc(s.order, 1)
                                j += 1
                    def onehots(g):
                        wait_past(v, s.scattered, g, 1, -7)
                        v.tensor_tensor(onehot[:, g.slot(8)], sb.iota[:, 0:W].unsqueeze(1).broadcast_to([P, TPG, W]),
                                        rel[:, bass.ds(g.times(TPG), TPG)].unsqueeze(2).broadcast_to([P, TPG, W]), ALU.is_equal).then_inc(s.onehot, 1)

                    g = t.back(3)
                    if g.exists() and soft:
                        v.wait_ge(s.factor_psum, g.times(1, 1))
                        wait_past(v, s.weights, g, 1, -1)
                        v.tensor_tensor(shifted[:, g.slot(2)], logits[:, g.slot(2)], maxima_bank.rearrange("p (t h) -> p t h", t=TPG),
                                        ALU.subtract).then_inc(s.shifted, 1)
                    if At(t.i, t.base + 1).exists() and layer != 2:
                        onehots(At(t.i, t.base + 1))
                    if g.exists() and soft and layer != 2:
                        wait_past(v, s.order, g, ORDER, FIRST - 3 * ORDER)
                        v.tensor_copy(factor_of[:, g.slot(4):g.slot(4) + 1], factor_bank).then_inc(s.factor_copied, 1)
                    g = t.back(1)
                    if g.exists() and layer == 0:
                        v.wait_ge(s.edge_term, g.times(1, 1))
                        v.wait_ge(s.gathered[g.slot(8)], g.uses(8, 16 * TPG))
                        wait_past(v, s.relued, g, 1, -1)
                        v.tensor_tensor(term[:, g.slot(2)], term_bank[g.slot(2)].rearrange("p (t n) -> p t n", t=TPG), rows[:, g.slot(8)], ALU.add).then_inc(s.term_read, 1)
                    if g.exists() and soft and layer != 2:
                        v.wait_ge(s.edge_term, g.times(1, 1))
                        v.wait_ge(s.gathered[g.slot(8)], g.uses(8, 16 * TPG))
                        wait_past(v, s.logits, g, 1, 0)
                        v.tensor_tensor(linear, term_bank[g.slot(2)][:, 0:TPG * H].rearrange("p (t h) -> p t h", t=TPG),
                                        rows[:, g.slot(8), :, D:D + H], ALU.add).then_inc(s.term_read, 1)
                    g = t.back(2)
                    if g.exists() and soft:
                        v.wait_ge(s.logits_lane, g.times(1, 1))
                        v.wait_ge(s.starts[g.slot(AHEAD)], g.uses(AHEAD, 16))
                        wait_past(v, s.factor_log, g, 1, 0)
                        before = running[:, 1 - g.slot(2), GE - 1:GE]
                        v.tensor_tensor_scan(running[:, g.slot(2)], starts[:, g.slot(AHEAD), 0:GE], lane_bank[0:H], before,
                                             ALU.add, ALU.max).then_inc(s.running, 1)
                    g = t.back(1)
                    if g.exists() and layer == 2:
                        v.wait_ge(s.relued, g.times(1, 1))
                        wait_past(v, s.logits, g, 1, -1)
                        v.scalar_tensor_tensor(term[:, g.slot(2)], term_bank[g.slot(2)].rearrange("p (t n) -> p t n", t=TPG), 0.2, relued[:, g.slot(2)],
                                               ALU.mult, ALU.add).then_inc(s.term_read, 1)
                    if g.exists() and soft and layer != 2:
                        v.wait_ge(s.term_read, g.times(1, 1))
                        wait_past(v, s.shifted, g, 1, -1)
                        v.scalar_tensor_tensor(logits[:, g.slot(2)], linear, 0.2, linear, ALU.mult, ALU.max).then_inc(s.logits, 1)
                    g = t.back(2)
                    if g.exists() and soft:
                        v.wait_ge(s.running, g.times(1, 1))
                        wait_past(v, s.maxima_psum, g, 1, -1)
                        v.tensor_tensor_scan(maxima[:, g.slot(2), ::-1], starts[:, g.slot(AHEAD), GE:0:-1], running[:, g.slot(2), ::-1],
                                             NEG, ALU.add, ALU.max).then_inc(s.lanes, 1)
                    g = t.back(3)
                    if g.exists() and soft:
                        v.wait_ge(s.weights, g.times(1, 1))
                        wait_past(v, s.scattered, g, 1, -1)
                        v.tensor_tensor(message[:, g.slot(2), :, 0:D].rearrange("p t (h c) -> p t h c", h=H),
                                        rows[:, g.slot(8), :, 0:D].rearrange("p t (h c) -> p t h c", h=H),
                                        message[:, g.slot(2), :, D:D + H].unsqueeze(3).broadcast_to([P, TPG, H, D // H]), ALU.mult).then_inc(s.message, 1)
                    g = t.back(2)
                    if g.exists() and soft and layer != 2:
                        v.wait_ge(s.lanes, g.times(1, 1))
                        wait_past(v, s.factor, g, 1, -1)
                        v.tensor_scalar(factor_log[:, g.slot(2):g.slot(2) + 1], running[:, 1 - g.slot(2), GE - 1:GE], maxima[:, g.slot(2), 0:1], 0.0,
                                        ALU.subtract, ALU.min).then_inc(s.factor_log, 1)
                    g = t.back(1)
                    if g.exists() and layer == 2:
                        v.wait_ge(s.term_read, g.times(1, 1))
                        v.tensor_tensor(term[:, g.slot(2)], term[:, g.slot(2)], sb.L2_att.unsqueeze(1).broadcast_to([P, TPG, D]), ALU.mult).then_inc(s.leaky, 1)
                    if g.exists() and layer == 2:
                        v.wait_ge(s.leaky, g.times(1, 1))
                        wait_past(v, s.shifted, g, 1, -1)
                        v.tensor_reduce(logits[:, g.slot(2)], term[:, g.slot(2)].rearrange("p t (h c) -> p t h c", h=H), AX, ALU.add).then_inc(s.logits, 1)

                sweep(nc, v, -1, 7, G - 2, G + 4, step)
    phase_end(nc, s)


def mlp0_phase(nc, io, sb):
    s = sems(nc, "mlp0", "scale", "stat", "act_stat", in_=2, up=2, up_done=2, down=2, down_done=2)
    with ExitStack() as ctx:
        tile = node_phase(nc, "mlp0", ctx)
        one_eps = tile("one_eps", [P, 1])
        hin = tile("hin", [P, 2, GE])
        mid = tile("mid", [P, 2, GE])
        square = tile("square", [P, N])
        st = tile("st", [P, 8])
        y = sb.sums
        up_bank = [sb.psum[:, k, :] for k in range(2)]
        down_bank = [sb.psum[:, 2 + k, :] for k in range(2)]
        with nc.Block() as block:
            @block.vector
            def _(v):
                v.tensor_scalar(one_eps, sb.L0_eps, 1.0, None, ALU.add).then_inc(s.scale, 1)
                v.wait_ge(s.scale, 1)

                def combine(c):
                    k = c.slot(2)
                    freed(v, s.up, c)
                    v.scalar_tensor_tensor(hin[:, k], sb.hT[:, nodes_of(c)], one_eps, sb.sums[:, nodes_of(c)], ALU.mult, ALU.add).then_inc(s.in_[k], 1)

                chunks(nc, v, [combine])
                v.wait_ge(s.down_done[0], CH - CH // 2)
                v.wait_ge(s.down_done[1], CH // 2)
                v.tensor_reduce(st[:, 0:1], y[:, 0:N], AX, ALU.add).then_inc(s.stat, 1)
                v.wait_ge(s.stat, 1)
                v.tensor_scalar(st[:, 1:2], st[:, 0:1], -1.0 / N, None, ALU.mult).then_inc(s.stat, 1)
                v.wait_ge(s.act_stat, 1)
                v.tensor_scalar(st[:, 3:4], st[:, 2:3], 1.0 / N, LN_EPS, ALU.mult, ALU.add).then_inc(s.stat, 1)
                v.wait_ge(s.act_stat, 2)
                v.reciprocal(st[:, 5:6], st[:, 4:5]).then_inc(s.stat, 1)
                v.wait_ge(s.stat, 4)
                v.tensor_tensor(sb.bn_scale, st[:, 5:6], sb.L0_gamma, ALU.mult).then_inc(s.stat, 1)
                v.wait_ge(s.stat, 5)
                v.scalar_tensor_tensor(sb.bn_shift, sb.bn_scale, st[:, 1:2], sb.L0_beta, ALU.mult, ALU.add).then_inc(s.stat, 1)

            @block.tensor
            def _(pe):
                def up(c):
                    k = c.slot(2)
                    pe.wait_ge(s.in_[k], c.nth())
                    freed(pe, s.up_done, c)
                    pe.matmul(up_bank[k], sb.L0_W1, hin[:, k], start=True, stop=True).then_inc(s.up[k], 1)

                def down(c):
                    k = c.slot(2)
                    pe.wait_ge(s.up_done[k], c.nth())
                    freed(pe, s.down_done, c)
                    pe.matmul(down_bank[k], sb.L0_W2, mid[:, k], start=True, stop=True).then_inc(s.down[k], 1)

                chunks(nc, pe, [up, down])

            @block.scalar
            def _(act):
                def relu(c):
                    k = c.slot(2)
                    act.wait_ge(s.up[k], c.nth())
                    freed(act, s.down, c)
                    act.activation(mid[:, k], up_bank[k], ACT.Relu, bias=sb.L0_b1).then_inc(s.up_done[k], 1)

                def out(c):
                    k = c.slot(2)
                    act.wait_ge(s.down[k], c.nth())
                    settle(act)
                    act.activation(y[:, nodes_of(c)], down_bank[k], ACT.Identity, bias=sb.L0_b2).then_inc(s.down_done[k], 1)

                chunks(nc, act, [relu, out])
                act.wait_ge(s.stat, 2)
                act.wait_ge(s.down_done[0], CH - CH // 2)
                act.wait_ge(s.down_done[1], CH // 2)
                act.activation(square, y[:, 0:N], ACT.Square, bias=st[:, 1:2], accum_out=st[:, 2:3]).then_inc(s.act_stat, 1)
                act.wait_ge(s.stat, 3)
                act.activation(st[:, 4:5], st[:, 3:4], ACT.Sqrt).then_inc(s.act_stat, 1)
    phase_end(nc, s)


def norm1_phase(nc, io, sb):
    s = sems(nc, "norm1", "ones", bn=2, plus_h=2, back=2, x_new=2, ln=2, root=2, h=2, transposed=2, kept=2, stored=2)
    with ExitStack() as ctx:
        tile = node_phase(nc, "norm1", ctx)
        norm = LayerNorm(tile, "ln", s.ln, s.root)
        z = tile("z", [P, 2, GE])
        zh = tile("zh", [P, 2, GE])
        rows = tile("rows", [P, 2, TPG, D + 1])
        back_bank = [sb.psum[:, k, :] for k in range(2)]
        h_bank = [sb.psum[:, 2 + k, :] for k in range(2)]
        with nc.Block() as block:
            @block.scalar
            def _(act):
                def batch_norm(c):
                    k = c.slot(2)
                    freed(act, s.plus_h, c)
                    settle(act)
                    act.activation(z[:, k], sb.sums[:, nodes_of(c)], ACT.Relu, bias=sb.bn_shift, scale=sb.bn_scale).then_inc(s.bn[k], 1)

                def normalise(c):
                    freed(act, s.transposed, c)
                    freed(act, s.stored, c, 16)
                    settle(act)
                    norm.apply(act, c, rows[:, c.slot(2), :, 0:D], blocks_of(sb, c), ACT.Relu, s.h)

                def keep(c):
                    k = c.slot(2)
                    act.wait_ge(s.transposed[k], c.nth())
                    act.wait_ge(s.plus_h[k], c.nth())
                    settle(act)
                    act.activation(sb.hT[:, nodes_of(c)], h_bank[k], ACT.Copy).then_inc(s.kept[k], 1)

                chunks(nc, act, [batch_norm, lambda c: norm.take_root(act, c), normalise, keep])

            @block.vector
            def _(v):
                v.memset(rows[:, :, :, D:D + 1], 1.0).then_inc(s.ones, 1)

                def plus_h(c):
                    k = c.slot(2)
                    v.wait_ge(s.bn[k], c.nth())
                    freed(v, s.back, c)
                    v.tensor_tensor(zh[:, k], z[:, k], sb.hT[:, nodes_of(c)], ALU.add).then_inc(s.plus_h[k], 1)

                def to_x(c):
                    k = c.slot(2)
                    v.wait_ge(s.back[k], c.nth())
                    x = blocks_of(sb, c)
                    v.tensor_tensor(x, x, back_bank[k].rearrange("p (b f) -> p b f", b=TPG), ALU.add).then_inc(s.x_new[k], 1)

                def statistics(c):
                    v.wait_ge(s.x_new[c.slot(2)], c.nth())
                    norm.statistics(v, c, blocks_of(sb, c), s.h)

                chunks(nc, v, [plus_h, to_x, statistics, lambda c: norm.scale_shift(v, c)])

            @block.tensor
            def _(pe):
                def back(c):
                    k = c.slot(2)
                    pe.wait_ge(s.plus_h[k], c.nth())
                    freed(pe, s.x_new, c)
                    flip(pe, lambda b: back_bank[k][:, piece(b)], lambda b: zh[:, k, piece(b)], sb.ident).then_inc(s.back[k], 1)

                def transpose(c):
                    k = c.slot(2)
                    pe.wait_ge(s.h[k], c.nth())
                    freed(pe, s.kept, c)
                    flip(pe, lambda b: h_bank[k][:, piece(b)], lambda b: rows[:, k, b, 0:D], sb.ident).then_inc(s.transposed[k], 1)

                chunks(nc, pe, [back, transpose])

            @block.sync
            def _(sp):
                sp.wait_ge(s.ones, 1)

                def store(c):
                    k = c.slot(2)
                    sp.wait_ge(s.h[k], c.nth())
                    sp.dma_start(table_rows(io.table1, c), rows[:, k]).then_inc(s.stored[k], 16)

                chunks(nc, sp, [store])
                sp.wait_ge(s.stored[0], 16 * (CH - CH // 2))
                sp.wait_ge(s.stored[1], 16 * (CH // 2))
    phase_end(nc, s)


def layer1_phase(nc, io, sb):
    s = sems(nc, "layer1", staged=2, products=2, degree=2, inverse=2, alone=2, mean=2, own=2, summed=2, x_new=2, ln=2, root=2,
             h=2, transposed=2, copied=2, proj=2, rows=2, stored=2)
    with ExitStack() as ctx:
        tile = node_phase(nc, "layer1", ctx)
        norm = LayerNorm(tile, "ln", s.ln, s.root)
        h_in = tile("h_in", [P, 2, GE])
        sum_in = tile("sum_in", [P, 2, GE])
        degree_in = tile("degree_in", [1, 2, GE])
        degree = tile("degree", [P, 2, TPG])
        inverse = tile("inverse", [P, 2, TPG])
        alone = tile("alone", [P, 2, TPG])
        mean = tile("mean", [P, 2, TPG, D])
        h = tile("h", [P, 2, TPG, D])
        h_out = tile("h_out", [P, 2, GE])
        rows = tile("rows", [P, 2, TPG, 2 * D])

        def bank(k, j):
            return sb.psum[:, 4 * k + j, :]

        def blocks(bank_of):
            return bank_of.rearrange("p (b f) -> p b f", b=TPG)

        proj = [sb.psum[:, 4 * k + 2:4 * k + 4, :].rearrange("p a (b f) -> p (a b) f", b=2) for k in range(2)]
        with nc.Block() as block:
            @block.scalar
            def _(act):
                def stage(c):
                    k = c.slot(2)
                    freed(act, s.products, c)
                    settle(act)
                    act.activation(h_in[:, k], sb.hT[:, nodes_of(c)], ACT.Copy)
                    act.activation(sum_in[:, k], sb.sums[:, nodes_of(c)], ACT.Copy)
                    act.activation(degree_in[:, k], sb.weight_sums[0:1, nodes_of(c)], ACT.Copy).then_inc(s.staged[k], 1)

                def neighbours(c):
                    k = c.slot(2)
                    act.wait_ge(s.inverse[k], c.nth())
                    freed(act, s.summed, c)
                    for b in range(TPG):
                        last = act.activation(mean[:, k, b, :], bank(k, 1)[:, piece(b)], ACT.Copy, scale=inverse[:, k, b:b + 1])
                    last.then_inc(s.mean[k], 1)

                def normalise(c):
                    freed(act, s.transposed, c)
                    norm.apply(act, c, h[:, c.slot(2)], blocks_of(sb, c), ACT.Relu, s.h)

                def keep(c):
                    k = c.slot(2)
                    act.wait_ge(s.transposed[k], c.nth())
                    act.wait_ge(s.staged[k], c.nth())
                    freed(act, s.proj, c)
                    settle(act)
                    act.activation(sb.hT[:, nodes_of(c)], bank(k, 1), ACT.Copy)
                    act.activation(h_out[:, k], bank(k, 1), ACT.Copy).then_inc(s.copied[k], 1)

                chunks(nc, act, [stage, neighbours, lambda c: norm.take_root(act, c), normalise, keep])

            @block.tensor
            def _(pe):
                def products(c):
                    k = c.slot(2)
                    pe.wait_ge(s.staged[k], c.nth())
                    freed(pe, s.rows, c)
                    freed(pe, s.copied, c)
                    for b in range(TPG):
                        pe.matmul(bank(k, 0)[:, piece(b)], sb.ones_row, sb.L1_b, start=True, stop=False)
                        pe.matmul(bank(k, 0)[:, piece(b)], h_in[:, k, piece(b)], sb.L1_W[:, 0, :], start=False, stop=True)
                        pe.matmul(bank(k, 1)[:, piece(b)], sum_in[:, k, piece(b)], sb.L1_W[:, 1, :], start=True, stop=True)
                        pe.matmul(bank(k, 2)[:, piece(b)], h_in[:, k, piece(b)], sb.L1_W[:, 1, :], start=True, stop=True)
                        last = pe.transpose(bank(k, 3)[:, b:b + 1], degree_in[:, k, piece(b)], sb.ident[0:1, 0:1])
                    last.then_inc(s.products[k], 1)

                def transpose(c):
                    k = c.slot(2)
                    pe.wait_ge(s.h[k], c.nth())
                    pe.wait_ge(s.mean[k], c.nth())
                    flip(pe, lambda b: bank(k, 1)[:, piece(b)], lambda b: h[:, k, b, :], sb.ident).then_inc(s.transposed[k], 1)

                def project(c):
                    k = c.slot(2)
                    pe.wait_ge(s.copied[k], c.nth())
                    pe.wait_ge(s.own[k], c.nth(TPG, TPG))
                    for b in range(TPG):
                        last = pe.matmul(proj[k][:, b, :], h_out[:, k, piece(b)], sb.L2_Wlr, start=True, stop=True)
                    last.then_inc(s.proj[k], 1)

                chunks(nc, pe, [products, transpose, project])

            @block.vector
            def _(v):
                def degrees(c):
                    k = c.slot(2)
                    v.wait_ge(s.products[k], c.nth())
                    freed(v, s.mean, c)
                    freed(v, s.own, c, TPG)
                    v.tensor_scalar(degree[:, k], bank(k, 3)[:, 0:TPG], 1.0, None, ALU.max).then_inc(s.degree[k], 1)
                    v.tensor_scalar(alone[:, k], bank(k, 3)[:, 0:TPG], 0.0, None, ALU.is_equal).then_inc(s.alone[k], 1)
                    v.wait_ge(s.degree[k], c.nth())
                    v.reciprocal(inverse[:, k], degree[:, k]).then_inc(s.inverse[k], 1)

                def combine(c):
                    k = c.slot(2)
                    v.wait_ge(s.mean[k], c.nth())
                    v.wait_ge(s.alone[k], c.nth())
                    for b in range(TPG):
                        v.scalar_tensor_tensor(mean[:, k, b, :], bank(k, 2)[:, piece(b)], alone[:, k, b:b + 1], mean[:, k, b, :],
                                               ALU.mult, ALU.add).then_inc(s.own[k], 1)
                    v.wait_ge(s.own[k], c.nth(TPG, TPG))
                    v.tensor_tensor(mean[:, k], mean[:, k], blocks(bank(k, 0)), ALU.add).then_inc(s.summed[k], 1)
                    v.wait_ge(s.summed[k], c.nth())
                    x = blocks_of(sb, c)
                    v.scalar_tensor_tensor(x, mean[:, k], 0.0, x, ALU.max, ALU.add).then_inc(s.x_new[k], 1)

                def statistics(c):
                    v.wait_ge(s.x_new[c.slot(2)], c.nth())
                    norm.statistics(v, c, blocks_of(sb, c), s.h)

                def rows_out(c):
                    k = c.slot(2)
                    v.wait_ge(s.proj[k], c.nth())
                    freed(v, s.stored, c, 32)
                    v.tensor_tensor(rows[:, k], proj[k], sb.L2_blr.unsqueeze(1).broadcast_to([P, TPG, 2 * D]), ALU.add).then_inc(s.rows[k], 1)

                chunks(nc, v, [degrees, combine, statistics, lambda c: norm.scale_shift(v, c), rows_out])

            @block.sync
            def _(sp):
                def store(c):
                    k = c.slot(2)
                    sp.wait_ge(s.rows[k], c.nth())
                    sp.dma_start(table_rows(io.table2, c), rows[:, k, :, 0:D]).then_inc(s.stored[k], 16)
                    sp.dma_start(table_rows(io.xr_table, c), rows[:, k, :, D:2 * D]).then_inc(s.stored[k], 16)

                chunks(nc, sp, [store])
                sp.wait_ge(s.stored[0], 32 * (CH - CH // 2))
                sp.wait_ge(s.stored[1], 32 * (CH // 2))
    phase_end(nc, s)


def ffn_phase(nc, io, sb):
    s = sems(nc, "ffn", staged=2, node_major=2, den=2, inverse=2, attn=2, plus_h=2, ln1=2, root1=2, norm1=2, gain1=2, hh=2,
             hhT_psum=2, hhT=2, up=2, gelu=2, down=2, res=2, ln2=2, root2=2, norm2=2, gain2=2, shift2=2, x_new=2, ln3=2,
             root3=2, h=2, hT_psum=2, h_out=2, proj=2, rows=2, stored=2)
    with ExitStack() as ctx:
        tile = node_phase(nc, "ffn", ctx)
        norm1 = LayerNorm(tile, "ln1", s.ln1, s.root1)
        norm2 = LayerNorm(tile, "ln2", s.ln2, s.root2)
        norm3 = LayerNorm(tile, "ln3", s.ln3, s.root3)
        sum_in = tile("sum_in", [P, 2, GE])
        den_in = tile("den_in", [8, 2, GE])
        h_in = tile("h_in", [P, 2, GE])
        den = tile("den", [P, 2, TPG, 8])
        attn = tile("attn", [P, 2, TPG, D])
        hh = tile("hh", [P, 2, TPG, D])
        hhT = tile("hhT", [P, 2, GE])
        gelu = tile("gelu", [P, 2, 4, GE])
        res = tile("res", [P, 2, TPG, D])
        h = tile("h", [P, 2, TPG, D])
        h_out = tile("h_out", [P, 2, GE])
        rows = tile("rows", [P, 2, TPG, D + 8])

        def bank(j):
            return sb.psum[:, j, :]

        def blocks(bank_of):
            return bank_of.rearrange("p (b f) -> p b f", b=TPG)

        def every_block(row):
            return row.unsqueeze(1).broadcast_to([P, TPG, D])

        proj = sb.psum[:, 6:8, :].rearrange("p a (b f) -> p (a b) f", b=2)[:, :, 0:D + 8]
        with nc.Block() as block:
            @block.scalar
            def _(act):
                def stage(c):
                    k = c.slot(2)
                    freed(act, s.node_major, c)
                    settle(act)
                    act.activation(sum_in[:, k], sb.sums[:, nodes_of(c)], ACT.Copy)
                    act.activation(den_in[:, k], sb.weight_sums[0:8, nodes_of(c)], ACT.Copy)
                    act.activation(h_in[:, k], sb.hT[:, nodes_of(c)], ACT.Identity, bias=sb.L2_batt).then_inc(s.staged[k], 1)

                def copy_hh(c):
                    k = c.slot(2)
                    act.wait_ge(s.hhT_psum[k], c.nth())
                    freed(act, s.up, c, 4)
                    act.activation(hhT[:, k], bank(0), ACT.Copy).then_inc(s.hhT[k], 1)

                def gelus(q):
                    def stage(c):
                        k = c.slot(2)
                        act.wait_ge(s.up[k], c.nth(q + 1, 4))
                        freed(act, s.down, c)
                        act.activation(gelu[:, k, q, :], bank(3 + q % 2), ACT.Gelu, bias=sb.L2_b1[:, q:q + 1]).then_inc(s.gelu[k], 1)
                    return stage

                def copy_h(c):
                    k = c.slot(2)
                    act.wait_ge(s.hT_psum[k], c.nth())
                    freed(act, s.proj, c)
                    act.activation(h_out[:, k], bank(6), ACT.Copy).then_inc(s.h_out[k], 1)

                def rows_out(c):
                    k = c.slot(2)
                    act.wait_ge(s.proj[k], c.nth())
                    freed(act, s.stored, c, 32)
                    act.activation(rows[:, k], proj, ACT.Copy).then_inc(s.rows[k], 1)

                def normalise1(c):
                    norm1.apply(act, c, attn[:, c.slot(2)], attn[:, c.slot(2)], ACT.Identity, s.norm1)

                def normalise2(c):
                    norm2.apply(act, c, res[:, c.slot(2)], res[:, c.slot(2)], ACT.Identity, s.norm2)

                def normalise3(c):
                    freed(act, s.hT_psum, c)
                    norm3.apply(act, c, h[:, c.slot(2)], blocks_of(sb, c), ACT.Relu, s.h)

                skewed(nc, act, 3, [
                    (0, 0.0, stage), (0, 6.5, lambda c: norm1.take_root(act, c)), (0, 7.3, normalise1), (0, 11.0, copy_hh),
                    (1, 0.9, gelus(0)), (1, 1.8, gelus(1)), (1, 2.7, gelus(2)), (1, 3.6, gelus(3)),
                    (2, 0.0, lambda c: norm2.take_root(act, c)), (2, 0.8, normalise2),
                    (2, 5.8, lambda c: norm3.take_root(act, c)), (2, 6.5, normalise3), (2, 8.6, copy_h), (2, 10.2, rows_out)])

            @block.tensor
            def _(pe):
                def to_nodes(c):
                    k = c.slot(2)
                    pe.wait_ge(s.staged[k], c.nth())
                    passed(pe, s.hhT, c)
                    flip(pe, lambda b: bank(0)[:, piece(b)], lambda b: sum_in[:, k, piece(b)], sb.ident)
                    flip(pe, lambda b: bank(1)[:, b * 8:(b + 1) * 8], lambda b: den_in[:, k, piece(b)], sb.ident, 8)
                    flip(pe, lambda b: bank(2)[:, piece(b)], lambda b: h_in[:, k, piece(b)], sb.ident).then_inc(s.node_major[k], 1)

                def flip_hh(c):
                    k = c.slot(2)
                    pe.wait_ge(s.hh[k], c.nth())
                    flip(pe, lambda b: bank(0)[:, piece(b)], lambda b: hh[:, k, b, :], sb.ident).then_inc(s.hhT_psum[k], 1)

                def ups(q):
                    def stage(c):
                        k = c.slot(2)
                        pe.wait_ge(s.hhT[k], c.nth())
                        if q >= 2:
                            pe.wait_ge(s.gelu[k], c.nth(q - 1, 4))
                        else:
                            passed(pe, s.gelu, c, 4)
                        pe.matmul(bank(3 + q % 2), sb.L2_W1[:, q * P:(q + 1) * P], hhT[:, k], start=True, stop=True).then_inc(s.up[k], 1)
                    return stage

                def down(c):
                    k = c.slot(2)
                    pe.wait_ge(s.gelu[k], c.nth(4, 4))
                    passed(pe, s.res, c)
                    for b in range(TPG):
                        pe.matmul(bank(5)[:, piece(b)], sb.ones_row, sb.L2_b2, start=True, stop=False)
                        for q in range(4):
                            last = pe.matmul(bank(5)[:, piece(b)], gelu[:, k, q, piece(b)], sb.L2_W2[:, q, :],
                                             start=False, stop=q == 3)
                    last.then_inc(s.down[k], 1)

                def flip_h(c):
                    k = c.slot(2)
                    pe.wait_ge(s.h[k], c.nth())
                    passed(pe, s.rows, c)
                    flip(pe, lambda b: bank(6)[:, piece(b)], lambda b: h[:, k, b, :], sb.ident).then_inc(s.hT_psum[k], 1)

                def project(c):
                    k = c.slot(2)
                    pe.wait_ge(s.h_out[k], c.nth())
                    for b in range(TPG):
                        last = pe.matmul(proj[:, b, :], h_out[:, k, piece(b)], sb.L3_W1x, start=True, stop=True)
                    last.then_inc(s.proj[k], 1)

                skewed(nc, pe, 3, [
                    (0, 1.5, to_nodes), (0, 10.5, flip_hh),
                    (1, 0.0, ups(0)), (1, 0.1, ups(1)), (1, 1.9, ups(2)), (1, 2.8, ups(3)), (1, 4.5, down),
                    (2, 8.0, flip_h), (2, 9.2, project)])

            @block.vector
            def _(v):
                def attention(c):
                    k = c.slot(2)
                    v.wait_ge(s.node_major[k], c.nth())
                    v.tensor_scalar(den[:, k], bank(1)[:, 0:8 * TPG].rearrange("p (b h) -> p b h", b=TPG), 1e-16, None, ALU.add).then_inc(s.den[k], 1)
                    v.wait_ge(s.den[k], c.nth())
                    v.reciprocal(den[:, k], den[:, k]).then_inc(s.inverse[k], 1)
                    v.wait_ge(s.inverse[k], c.nth())
                    freed(v, s.gain1, c)
                    v.tensor_tensor(attn[:, k].rearrange("p b (h c) -> p b h c", h=8),
                                    bank(0).rearrange("p (b h c) -> p b h c", b=TPG, h=8),
                                    den[:, k].unsqueeze(3).broadcast_to([P, TPG, 8, D // 8]), ALU.mult).then_inc(s.attn[k], 1)
                    v.wait_ge(s.attn[k], c.nth())
                    v.tensor_tensor(attn[:, k], attn[:, k], blocks(bank(2)), ALU.add).then_inc(s.plus_h[k], 1)

                def statistics1(c):
                    v.wait_ge(s.plus_h[c.slot(2)], c.nth())
                    norm1.statistics(v, c, attn[:, c.slot(2)], s.norm1)

                def scaled1(c):
                    k = c.slot(2)
                    v.wait_ge(s.norm1[k], c.nth())
                    freed(v, s.hhT_psum, c)
                    freed(v, s.res, c)
                    v.tensor_tensor(hh[:, k], attn[:, k], every_block(sb.L2_g1), ALU.mult).then_inc(s.gain1[k], 1)
                    v.wait_ge(s.gain1[k], c.nth())
                    v.tensor_tensor(hh[:, k], hh[:, k], every_block(sb.L2_be1), ALU.add).then_inc(s.hh[k], 1)

                def residual(c):
                    k = c.slot(2)
                    v.wait_ge(s.down[k], c.nth())
                    v.wait_ge(s.hh[k], c.nth())
                    freed(v, s.x_new, c)
                    v.tensor_tensor(res[:, k], blocks(bank(5)), hh[:, k], ALU.add).then_inc(s.res[k], 1)

                def statistics2(c):
                    v.wait_ge(s.res[c.slot(2)], c.nth())
                    norm2.statistics(v, c, res[:, c.slot(2)], s.norm2)

                def to_x(c):
                    k = c.slot(2)
                    x = blocks_of(sb, c)
                    v.wait_ge(s.norm2[k], c.nth())
                    v.tensor_tensor(res[:, k], res[:, k], every_block(sb.L2_g2), ALU.mult).then_inc(s.gain2[k], 1)
                    v.wait_ge(s.gain2[k], c.nth())
                    v.tensor_tensor(res[:, k], res[:, k], every_block(sb.L2_be2), ALU.add).then_inc(s.shift2[k], 1)
                    v.wait_ge(s.shift2[k], c.nth())
                    v.tensor_tensor(x, x, res[:, k], ALU.add).then_inc(s.x_new[k], 1)

                def statistics3(c):
                    v.wait_ge(s.x_new[c.slot(2)], c.nth())
                    norm3.statistics(v, c, blocks_of(sb, c), s.h)

                skewed(nc, v, 3, [
                    (0, 3.0, attention), (0, 5.0, statistics1), (0, 7.0, lambda c: norm1.scale_shift(v, c)), (0, 9.0, scaled1),
                    (1, 9.5, residual), (1, 10.2, statistics2),
                    (2, 0.5, lambda c: norm2.scale_shift(v, c)), (2, 2.4, to_x), (2, 4.3, statistics3),
                    (2, 6.2, lambda c: norm3.scale_shift(v, c))])

            @block.sync
            def _(sp):
                def store(c):
                    k = c.slot(2)
                    sp.wait_ge(s.rows[k], c.nth())
                    sp.dma_start(table_rows(io.table3, c), rows[:, k, :, 0:D + 4]).then_inc(s.stored[k], 16)
                    sp.dma_start(table_rows(io.adst3, c), rows[:, k, :, D + 4:D + 8]).then_inc(s.stored[k], 16)

                skewed(nc, sp, 3, [(2, 11.0, store)])
                sp.wait_ge(s.stored[0], 32 * (CH - CH // 2))
                sp.wait_ge(s.stored[1], 32 * (CH // 2))
    phase_end(nc, s)


def gat_out_phase(nc, io, sb, last_layer):
    s = sems(nc, f"gat{1 + last_layer}", "out", staged=2, node_major=2, den=2, inverse=2, ratio=2, biased=2, low=2, exp=2,
             relu=2, elu=2, eluT_psum=2, eluT=2, proj=2, rows=2, stored=2)
    H = 1 if last_layer else 4
    bias = sb.L3_b2 if last_layer else sb.L3_b1
    with ExitStack() as ctx:
        tile = node_phase(nc, f"gat{1 + last_layer}", ctx)
        sum_in = tile("sum_in", [P, 2, GE])
        den_in = tile("den_in", [H, 2, GE])
        den = tile("den", [P, 2, TPG, H])
        val = tile("val", [P, 2, TPG, D])
        low = tile("low", [P, 2, TPG, D])
        high = tile("high", [P, 2, TPG, D])
        elu = tile("elu", [P, 2, TPG, D])
        eluT = tile("eluT", [P, 2, GE])
        rows = tile("rows", [P, 2, TPG, D + 2])

        def bank(k, j):
            return sb.psum[:, 4 * k + j, :]

        proj = [sb.psum[:, 4 * k + 2:4 * k + 4, :].rearrange("p a (b f) -> p (a b) f", b=2)[:, :, 0:D + 2] for k in range(2)]
        with nc.Block() as block:
            @block.scalar
            def _(act):
                def stage(c):
                    k = c.slot(2)
                    freed(act, s.node_major, c)
                    settle(act)
                    act.activation(sum_in[:, k], sb.sums[:, nodes_of(c)], ACT.Copy)
                    act.activation(den_in[:, k], sb.weight_sums[0:H, nodes_of(c)], ACT.Copy).then_inc(s.staged[k], 1)

                def parts(c):
                    k = c.slot(2)
                    act.wait_ge(s.biased[k], c.nth())
                    freed(act, s.elu, c)
                    act.activation(high[:, k], val[:, k], ACT.Relu).then_inc(s.relu[k], 1)
                    act.wait_ge(s.low[k], c.nth())
                    act.activation(low[:, k], low[:, k], ACT.Exp).then_inc(s.exp[k], 1)

                def copy_elu(c):
                    k = c.slot(2)
                    act.wait_ge(s.eluT_psum[k], c.nth())
                    freed(act, s.proj, c)
                    act.activation(eluT[:, k], bank(k, 0), ACT.Copy).then_inc(s.eluT[k], 1)

                def rows_out(c):
                    k = c.slot(2)
                    act.wait_ge(s.proj[k], c.nth())
                    freed(act, s.stored, c, 32)
                    act.activation(rows[:, k], proj[k], ACT.Copy).then_inc(s.rows[k], 1)

                chunks(nc, act, [stage, parts] + ([] if last_layer else [copy_elu, rows_out]))

            @block.tensor
            def _(pe):
                def to_nodes(c):
                    k = c.slot(2)
                    pe.wait_ge(s.staged[k], c.nth())
                    freed(pe, s.ratio if last_layer else s.eluT, c)
                    flip(pe, lambda b: bank(k, 0)[:, piece(b)], lambda b: sum_in[:, k, piece(b)], sb.ident)
                    flip(pe, lambda b: bank(k, 1)[:, b * H:(b + 1) * H], lambda b: den_in[:, k, piece(b)], sb.ident, H).then_inc(s.node_major[k], 1)

                def flip_elu(c):
                    k = c.slot(2)
                    pe.wait_ge(s.elu[k], c.nth())
                    flip(pe, lambda b: bank(k, 0)[:, piece(b)], lambda b: elu[:, k, b, :], sb.ident).then_inc(s.eluT_psum[k], 1)

                def project(c):
                    k = c.slot(2)
                    pe.wait_ge(s.eluT[k], c.nth())
                    freed(pe, s.rows, c)
                    for b in range(TPG):
                        last = pe.matmul(proj[k][:, b, :], eluT[:, k, piece(b)], sb.L3_W2x, start=True, stop=True)
                    last.then_inc(s.proj[k], 1)

                chunks(nc, pe, [to_nodes] + ([] if last_layer else [flip_elu, project]))

            @block.vector
            def _(v):
                def ratio(c):
                    k = c.slot(2)
                    v.wait_ge(s.node_major[k], c.nth())
                    v.tensor_scalar(den[:, k], bank(k, 1)[:, 0:H * TPG].rearrange("p (b h) -> p b h", b=TPG), 1e-16, None, ALU.add).then_inc(s.den[k], 1)
                    v.wait_ge(s.den[k], c.nth())
                    v.reciprocal(den[:, k], den[:, k]).then_inc(s.inverse[k], 1)
                    v.wait_ge(s.inverse[k], c.nth())
                    freed(v, s.elu, c)
                    v.tensor_tensor(val[:, k].rearrange("p b (h c) -> p b h c", h=H),
                                    bank(k, 0).rearrange("p (b h c) -> p b h c", b=TPG, h=H),
                                    den[:, k].unsqueeze(3).broadcast_to([P, TPG, H, D // H]), ALU.mult).then_inc(s.ratio[k], 1)
                    v.wait_ge(s.ratio[k], c.nth())
                    v.tensor_tensor(val[:, k], val[:, k], bias.unsqueeze(1).broadcast_to([P, TPG, D]), ALU.add).then_inc(s.biased[k], 1)
                    v.wait_ge(s.biased[k], c.nth())
                    v.tensor_scalar(low[:, k], val[:, k], 0.0, None, ALU.min).then_inc(s.low[k], 1)

                def combine(c):
                    k = c.slot(2)
                    v.wait_ge(s.relu[k], c.nth())
                    v.wait_ge(s.exp[k], c.nth())
                    if not last_layer:
                        freed(v, s.eluT_psum, c)
                    elif c.i is not None or c.base >= 2:
                        v.wait_ge(s.out, c.times(1, -1))
                    v.scalar_tensor_tensor(elu[:, k], low[:, k], -1.0, high[:, k], ALU.add, ALU.add).then_inc(s.elu[k], 1)
                    if last_layer:
                        v.wait_ge(s.elu[k], c.nth())
                        x = blocks_of(sb, c)
                        v.tensor_tensor(x, x, elu[:, k], ALU.add).then_inc(s.out, 1)

                chunks(nc, v, [ratio, combine])

            @block.sync
            def _(sp):
                if last_layer:
                    whole = N // P
                    sp.wait_ge(s.out, CH)
                    sp.dma_start(io.out[0:whole * P, :].rearrange("(b p) f -> p b f", p=P), sb.x[:, 0:whole, :]).then_inc(s.stored[0], 16)
                    sp.dma_start(io.out[whole * P:N, :], sb.x[0:N - whole * P, whole, :]).then_inc(s.stored[0], 16)
                    sp.wait_ge(s.stored[0], 32)
                    return

                def store(c):
                    k = c.slot(2)
                    sp.wait_ge(s.rows[k], c.nth())
                    sp.dma_start(table_rows(io.table4, c), rows[:, k, :, 0:D + 1]).then_inc(s.stored[k], 16)
                    sp.dma_start(table_rows(io.adst4, c), rows[:, k, :, D:D + 2]).then_inc(s.stored[k], 16)

                chunks(nc, sp, [store])
                sp.wait_ge(s.stored[0], 32 * (CH - CH // 2))
                sp.wait_ge(s.stored[1], 32 * (CH // 2))
    phase_end(nc, s)


def build(nc, io):
    def dram(name, shape):
        return nc.dram_tensor(name, shape, F32, kind="Internal").ap()

    io = named(
        **io,
        starts=dram("segment_starts", (1, EP + 1)),
        table0=dram("table0", (NP, D)), table1=dram("table1", (NP, D + 1)),
        table2=dram("table2", (NP, D)), xr_table=dram("xr_table", (NP, D)),
        table3=dram("table3", (NP, D + 4)), adst3=dram("adst3", (NP, 4)),
        table4=dram("table4", (NP, D + 1)), adst4=dram("adst4", (NP, 2)),
    )
    with ExitStack() as ctx:
        def tile(name, shape, dt=F32):
            return ctx.enter_context(nc.sbuf_tensor(name, shape, dt))[:]

        sb = named(
            x=tile("x_nodes", [P, NP // P, D]), hT=tile("hT", [P, NP]), sums=tile("sums", [P, NP]),
            weight_sums=tile("weight_sums", [8, NP]),
            ident=tile("ident", [P, P]), iota=tile("iota", [P, P]), mask4=tile("mask4", [P, 4]),
            expand8=tile("expand8", [8, P]), expand4=tile("expand4", [4, P]), ones_row=tile("ones_row", [1, P]),
            window_row=tile("window_row", [1, T], I32), rel_tile=tile("rel_tile", [P, T]),
            rel_group=tile("rel_group", [P, T]), narrow=tile("narrow", [1, 1], I32),
            L0_We=tile("L0_We", [64, D]), L0_W1=tile("L0_W1", [P, D]), L0_W2=tile("L0_W2", [P, D]),
            L0_b1=tile("L0_b1", [P, 1]), L0_b2=tile("L0_b2", [P, 1]), L0_gamma=tile("L0_gamma", [P, 1]),
            L0_beta=tile("L0_beta", [P, 1]), L0_be=tile("L0_be", [P, D]), L0_eps=tile("L0_eps", [P, 1]),
            bn_scale=tile("bn_scale", [P, 1]), bn_shift=tile("bn_shift", [P, 1]),
            L1_W=tile("L1_W", [P, 2, D]), L1_b=tile("L1_b", [1, D]),
            L2_Wlr=tile("L2_Wlr", [P, 2 * D]), L2_blr=tile("L2_blr", [P, 2 * D]), L2_We=tile("L2_We", [P, D]),
            L2_att=tile("L2_att", [P, D]), L2_batt=tile("L2_batt", [P, 1]),
            L2_W1=tile("L2_W1", [P, 4 * D]), L2_b1=tile("L2_b1", [P, 4]), L2_W2=tile("L2_W2", [P, 4, D]),
            L2_b2=tile("L2_b2", [1, D]), L2_g1=tile("L2_g1", [P, D]), L2_be1=tile("L2_be1", [P, D]),
            L2_g2=tile("L2_g2", [P, D]), L2_be2=tile("L2_be2", [P, D]),
            L3_W1x=tile("L3_W1x", [P, D + 8]), L3_W2x=tile("L3_W2x", [P, D + 2]),
            L3_b1=tile("L3_b1", [P, D]), L3_b2=tile("L3_b2", [P, D]),
            psum=ctx.enter_context(nc.psum_tensor("psum", [P, 8, GE], F32))[:],
        )
        setup_phase(nc, io, sb)
        norm0_phase(nc, io, sb)
        edge_phase(nc, io, sb, 0)
        mlp0_phase(nc, io, sb)
        norm1_phase(nc, io, sb)
        edge_phase(nc, io, sb, 1)
        layer1_phase(nc, io, sb)
        edge_phase(nc, io, sb, 2)
        ffn_phase(nc, io, sb)
        edge_phase(nc, io, sb, 3)
        gat_out_phase(nc, io, sb, False)
        edge_phase(nc, io, sb, 4)
        gat_out_phase(nc, io, sb, True)


def laid_out(a):
    def pad_rows(x, n, value=0):
        out = np.full((n,) + x.shape[1:], value, x.dtype)
        out[:x.shape[0]] = x
        return out

    src = pad_rows(np.asarray(a["src"]), EP)
    dst = pad_rows(np.asarray(a["dst"]), EP, N)
    heads = {h: np.kron(np.eye(h, dtype=np.float32), np.ones((D // h, 1), np.float32)) for h in (4, 8)}
    col = lambda x: np.asarray(x).reshape(-1, 1)
    row = lambda x: np.asarray(x).reshape(-1)
    att = lambda n: np.stack([np.asarray(a[f"L3_gnn_att_src{n}"]).reshape(-1), np.asarray(a[f"L3_gnn_att_dst{n}"]).reshape(-1)], 1)
    return {
        "x": pad_rows(np.asarray(a["x"]), NP),
        "src_g": src.reshape(G, TPG, P).transpose(0, 2, 1),
        "dst_t": dst.reshape(T, P).T,
        "window": dst[::P].reshape(1, T),
        "dst_row": np.concatenate([np.full(1, -1, dst.dtype), dst]).reshape(1, EP + 1),
        "ea64T": pad_rows(np.asarray(a["edge_attr_64"]), EP).T,
        "ea128T": pad_rows(np.asarray(a["edge_attr_128"]), EP).T,
        "ident": np.eye(P, dtype=np.float32),
        "iota": np.tile(np.arange(P, dtype=np.float32), (P, 1)),
        "mask4": heads[4], "expand8": heads[8].T, "expand4": heads[4].T,
        "ones_row": np.ones((1, P), np.float32),
        "L0_We": a["L0_gnn_We"], "L0_W1": a["L0_gnn_W1"], "L0_W2": a["L0_gnn_W2"],
        "L0_b1": col(a["L0_gnn_b1"]), "L0_b2": col(a["L0_gnn_b2"]), "L0_gamma": col(a["L0_gnn_gamma"]),
        "L0_beta": col(a["L0_gnn_beta"]), "L0_be": row(a["L0_gnn_be"]), "L0_eps": row(a["L0_gnn_eps"]),
        "L1_WT": np.asarray(a["L1_gnn_W"]).T, "L1_b": np.asarray(a["L1_gnn_b"]).reshape(1, -1),
        "L2_Wl": a["L2_gnn_W_l"], "L2_Wr": a["L2_gnn_W_r"], "L2_We": a["L2_gnn_W_e"],
        "L2_bl": row(a["L2_gnn_b_l"]), "L2_br": row(a["L2_gnn_b_r"]), "L2_att": row(a["L2_gnn_att"]),
        "L2_batt": col(a["L2_gnn_b_att"]), "L2_W1": a["L2_gnn_W1"], "L2_b1": np.asarray(a["L2_gnn_b1"]).reshape(4, P).T, "L2_W2": a["L2_gnn_W2"],
        "L2_b2": np.asarray(a["L2_gnn_b2"]).reshape(1, -1), "L2_g1": row(a["L2_gnn_g1"]), "L2_be1": row(a["L2_gnn_be1"]),
        "L2_g2": row(a["L2_gnn_g2"]), "L2_be2": row(a["L2_gnn_be2"]),
        "L3_W1": a["L3_gnn_W1"], "L3_W1T": np.asarray(a["L3_gnn_W1"]).T, "L3_W2": a["L3_gnn_W2"],
        "L3_W2T": np.asarray(a["L3_gnn_W2"]).T, "L3_att1": att(1), "L3_att2": att(2),
        "L3_b1": row(a["L3_gnn_b1"]), "L3_b2": row(a["L3_gnn_b2"]),
    }


def kernel(**inputs):
    import concourse.bacc as bacc
    from concourse.bass_utils import run_bass_kernel_spmd

    nc = bacc.Bacc("TRN2", target_bir_lowering=False, num_devices=1)
    arrays, io = {}, {}
    for name, value in laid_out(inputs).items():
        value = np.ascontiguousarray(value)
        arrays[f"in_{name}"] = value
        io[name] = nc.dram_tensor(f"in_{name}", value.shape, mybir.dt.from_np(value.dtype), kind="ExternalInput").ap()
    io["out"] = nc.dram_tensor("out_0", (N, D), F32, kind="ExternalOutput").ap()
    build(nc, io)
    result = run_bass_kernel_spmd(nc, [arrays], core_ids=[0])
    return result.results[0]["out_0"]
```
